# Optimizing a Trainium2 kernel written in Bass

```python
import numpy as np
import jax
import jax.numpy as jnp

def _softmax(x, axis=-1):
    return jax.nn.softmax(x, axis=axis)

def _gelu(x):
    return jax.nn.gelu(x, approximate=True)

def _silu(x):
    return jax.nn.silu(x)

def _sigmoid(x):
    return jax.nn.sigmoid(x)

def _layernorm(x, axis=-1, eps=1e-05):
    m = jnp.mean(x, axis=axis, keepdims=True)
    v = jnp.var(x, axis=axis, keepdims=True)
    return (x - m) / jnp.sqrt(v + eps)

def _scatter_add(tgt, idx, src, axis=0):
    return tgt.at[idx].add(src)

def _segment_sum(src, seg, n):
    return jax.ops.segment_sum(src, seg, n)
kernel_name = 'mk_xattn_ffn_d1_seqx_r8_7290b5'

def setup_inputs(seed: int=0):
    np.random.seed(seed)
    _w = jnp.asarray

    def _rec_inputs():
        import jax
        import jax.numpy as jnp
        _rk = jax.random.key(seed)
        x = 7.22e-05 + 1 * jax.random.normal(jax.random.fold_in(_rk, 1), (64, 64, 128), jnp.float32)
        _lenS = 64 - jax.random.randint(jax.random.fold_in(_rk, 7), (64,), 0, max(1, 64 // 4) + 1, jnp.int32)
        _lenS2 = 64 - jax.random.randint(jax.random.fold_in(_rk, 8), (64,), 0, max(1, 64 // 4) + 1, jnp.int32)
        _ctx_1024P = jax.random.normal(jax.random.fold_in(_rk, 11), (64, 16, 128), jnp.float32)
        _ctx_1024c = jax.random.dirichlet(jax.random.fold_in(_rk, 511), 0.3 * jnp.ones((16,), jnp.float32), (64, 64))
        _ctx_1024t = jnp.einsum('bsk,bkd->bsd', _ctx_1024c, _ctx_1024P)
        _ctx_1024t = _ctx_1024t * jax.lax.rsqrt(jnp.mean(jnp.square(_ctx_1024t)) + 1e-12) * 0.953939
        ctx_1024 = -1.39393e-06 + 0.999914 * (_ctx_1024t + 0.3 * jax.random.normal(jax.random.fold_in(_rk, 611), (64, 64, 128), jnp.float32))
        return (x, ctx_1024)
    x, ctx_1024 = _rec_inputs()

    def _L0_xattn_setup():
        import jax, jax.numpy as jnp
        import numpy as np
        DIM = 128
        CTX_DIM = 128
        HEADS = 16
        DIM_HEAD = 64
        INNER = HEADS * DIM_HEAD
        FF_INNER = 4 * DIM
        EPS = 1e-05

        def layer_norm(x, g, b):
            mu = jnp.mean(x, axis=-1, keepdims=True)
            var = jnp.var(x, axis=-1, keepdims=True)
            return (x - mu) * jax.lax.rsqrt(var + EPS) * g + b
        key = jax.random.key(seed)
        ks = jax.random.split(key, 9)
        b, n, j = (4, 256, 128)
        inp = {'x': jax.random.normal(ks[0], (b, n, DIM), dtype=jnp.float32), 'context': jax.random.normal(ks[1], (b, j, CTX_DIM), dtype=jnp.float32), 'ln_g': jnp.ones((DIM,), jnp.float32), 'ln_b': jnp.zeros((DIM,), jnp.float32), 'cln_g': jnp.ones((CTX_DIM,), jnp.float32), 'cln_b': jnp.zeros((CTX_DIM,), jnp.float32), 'Wq': jax.random.normal(ks[2], (DIM, INNER), dtype=jnp.float32) * DIM ** (-0.5), 'Wkv': jax.random.normal(ks[3], (CTX_DIM, 2 * DIM_HEAD), dtype=jnp.float32) * CTX_DIM ** (-0.5), 'Wo': jax.random.normal(ks[4], (INNER, DIM), dtype=jnp.float32) * INNER ** (-0.5), 'Wff1': jax.random.normal(ks[5], (DIM, 2 * FF_INNER), dtype=jnp.float32) * DIM ** (-0.5), 'Wff2': jax.random.normal(ks[6], (FF_INNER, DIM), dtype=jnp.float32) * FF_INNER ** (-0.5)}
        return inp
    _L0_xattn_all = _L0_xattn_setup()
    _L0_xattn_in = {k: v for k, v in _L0_xattn_all.items() if k in ('ln_g', 'ln_b', 'cln_g', 'cln_b', 'Wq', 'Wkv', 'Wo', 'Wff1', 'Wff2')}
    del _L0_xattn_all

    def _L0_ffn_setup():
        import jax, jax.numpy as jnp
        import numpy as np
        B, S, H, NH, E, F = (4, 128, 128, 16, 8, 512)
        D = H // NH
        EPS = 1e-05

        def _layernorm(x, g, b):
            mu = jnp.mean(x, axis=-1, keepdims=True)
            var = jnp.var(x, axis=-1, keepdims=True)
            return (x - mu) * jax.lax.rsqrt(var + EPS) * g + b
        key = jax.random.key(seed)
        ks = jax.random.split(key, 16)
        s = 0.02
        return {'x': jax.random.normal(ks[0], (B, S, H), jnp.float32), 'ln1_g': jnp.ones((H,), jnp.float32), 'ln1_b': jnp.zeros((H,), jnp.float32), 'ln2_g': jnp.ones((H,), jnp.float32), 'ln2_b': jnp.zeros((H,), jnp.float32), 'wq': jax.random.normal(ks[1], (H, H), jnp.float32) * s, 'bq': jnp.zeros((H,), jnp.float32), 'wk': jax.random.normal(ks[2], (H, H), jnp.float32) * s, 'bk': jnp.zeros((H,), jnp.float32), 'wv': jax.random.normal(ks[3], (H, H), jnp.float32) * s, 'bv': jnp.zeros((H,), jnp.float32), 'wo': jax.random.normal(ks[4], (H, H), jnp.float32) * s, 'bo': jnp.zeros((H,), jnp.float32), 'gate_w': jax.random.normal(ks[5], (H, E), jnp.float32) * s, 'gate_b': jnp.zeros((E,), jnp.float32), 'w1': jax.random.normal(ks[6], (E, H, F), jnp.float32) * s, 'b1': jnp.zeros((E, F), jnp.float32), 'w2': jax.random.normal(ks[7], (E, F, H), jnp.float32) * s, 'b2': jnp.zeros((E, H), jnp.float32)}
    _L0_ffn_all = _L0_ffn_setup()
    _L0_ffn_in = {k: v for k, v in _L0_ffn_all.items() if k in ('ln1_g', 'ln1_b', 'ln2_g', 'ln2_b', 'wq', 'bq', 'wk', 'bk', 'wv', 'bv', 'wo', 'bo', 'gate_w', 'gate_b', 'w1', 'b1', 'w2', 'b2')}
    del _L0_ffn_all
    return {'x': x, 'ctx_1024': ctx_1024, 'L0_xattn_ln_g': _L0_xattn_in['ln_g'], 'L0_xattn_ln_b': _L0_xattn_in['ln_b'], 'L0_xattn_cln_g': _L0_xattn_in['cln_g'], 'L0_xattn_cln_b': _L0_xattn_in['cln_b'], 'L0_xattn_Wq': _L0_xattn_in['Wq'], 'L0_xattn_Wkv': _L0_xattn_in['Wkv'], 'L0_xattn_Wo': _L0_xattn_in['Wo'], 'L0_xattn_Wff1': _L0_xattn_in['Wff1'], 'L0_xattn_Wff2': _L0_xattn_in['Wff2'], 'L0_ffn_ln1_g': _L0_ffn_in['ln1_g'], 'L0_ffn_ln1_b': _L0_ffn_in['ln1_b'], 'L0_ffn_ln2_g': _L0_ffn_in['ln2_g'], 'L0_ffn_ln2_b': _L0_ffn_in['ln2_b'], 'L0_ffn_wq': _L0_ffn_in['wq'], 'L0_ffn_bq': _L0_ffn_in['bq'], 'L0_ffn_wk': _L0_ffn_in['wk'], 'L0_ffn_bk': _L0_ffn_in['bk'], 'L0_ffn_wv': _L0_ffn_in['wv'], 'L0_ffn_bv': _L0_ffn_in['bv'], 'L0_ffn_wo': _L0_ffn_in['wo'], 'L0_ffn_bo': _L0_ffn_in['bo'], 'L0_ffn_gate_w': _L0_ffn_in['gate_w'], 'L0_ffn_gate_b': _L0_ffn_in['gate_b'], 'L0_ffn_w1': _L0_ffn_in['w1'], 'L0_ffn_b1': _L0_ffn_in['b1'], 'L0_ffn_w2': _L0_ffn_in['w2'], 'L0_ffn_b2': _L0_ffn_in['b2']}

def reference(x, ctx_1024, L0_xattn_ln_g, L0_xattn_ln_b, L0_xattn_cln_g, L0_xattn_cln_b, L0_xattn_Wq, L0_xattn_Wkv, L0_xattn_Wo, L0_xattn_Wff1, L0_xattn_Wff2, L0_ffn_ln1_g, L0_ffn_ln1_b, L0_ffn_ln2_g, L0_ffn_ln2_b, L0_ffn_wq, L0_ffn_bq, L0_ffn_wk, L0_ffn_bk, L0_ffn_wv, L0_ffn_bv, L0_ffn_wo, L0_ffn_bo, L0_ffn_gate_w, L0_ffn_gate_b, L0_ffn_w1, L0_ffn_b1, L0_ffn_w2, L0_ffn_b2):
    import jax
    import jax.numpy as jnp

    def _L0_xattn_ref(x, context, ln_g, ln_b, cln_g, cln_b, Wq, Wkv, Wo, Wff1, Wff2):
        import jax, jax.numpy as jnp
        import numpy as np
        DIM = 128
        CTX_DIM = 128
        HEADS = 16
        DIM_HEAD = 64
        INNER = HEADS * DIM_HEAD
        FF_INNER = 4 * DIM
        EPS = 1e-05

        def layer_norm(x, g, b):
            mu = jnp.mean(x, axis=-1, keepdims=True)
            var = jnp.var(x, axis=-1, keepdims=True)
            return (x - mu) * jax.lax.rsqrt(var + EPS) * g + b
        scale = DIM_HEAD ** (-0.5)
        xn = layer_norm(x, ln_g, ln_b)
        cn = layer_norm(context, cln_g, cln_b)
        b, n, _ = xn.shape
        q = (xn @ Wq).reshape(b, n, HEADS, DIM_HEAD).transpose(0, 2, 1, 3) * scale
        kv = cn @ Wkv
        k, v = (kv[..., :DIM_HEAD], kv[..., DIM_HEAD:])
        sim = jnp.einsum('bhid,bjd->bhij', q, k)
        attn = jax.nn.softmax(sim, axis=-1)
        out = jnp.einsum('bhij,bjd->bhid', attn, v)
        out = out.transpose(0, 2, 1, 3).reshape(b, n, INNER) @ Wo
        ff = xn @ Wff1
        h, gate = (ff[..., :FF_INNER], ff[..., FF_INNER:])
        out = out + jax.nn.silu(gate) * h @ Wff2
        return out

    def _L0_ffn_ref(x, ln1_g, ln1_b, ln2_g, ln2_b, wq, bq, wk, bk, wv, bv, wo, bo, gate_w, gate_b, w1, b1, w2, b2):
        import jax, jax.numpy as jnp
        import numpy as np
        B, S, H, NH, E, F = (4, 128, 128, 16, 8, 512)
        D = H // NH
        EPS = 1e-05

        def _layernorm(x, g, b):
            mu = jnp.mean(x, axis=-1, keepdims=True)
            var = jnp.var(x, axis=-1, keepdims=True)
            return (x - mu) * jax.lax.rsqrt(var + EPS) * g + b
        b, s, h = x.shape
        hn = _layernorm(x, ln1_g, ln1_b)
        q = (hn @ wq + bq).reshape(b, s, NH, D).transpose(0, 2, 1, 3)
        k = (hn @ wk + bk).reshape(b, s, NH, D).transpose(0, 2, 1, 3)
        v = (hn @ wv + bv).reshape(b, s, NH, D).transpose(0, 2, 1, 3)
        scores = jnp.einsum('bhqd,bhkd->bhqk', q, k) / jnp.sqrt(jnp.float32(D))
        attn = jax.nn.softmax(scores, axis=-1)
        o = jnp.einsum('bhqk,bhkd->bhqd', attn, v)
        o = o.transpose(0, 2, 1, 3).reshape(b, s, h)
        x = x + (o @ wo + bo)
        hn2 = _layernorm(x, ln2_g, ln2_b).reshape(-1, h)
        logits = hn2 @ gate_w + gate_b
        idx = jnp.argmax(logits, axis=-1)
        mid = jax.nn.relu(jnp.einsum('th,ehf->etf', hn2, w1) + b1[:, None, :])
        y = jnp.einsum('etf,efh->eth', mid, w2) + b2[:, None, :]
        moe = y[idx, jnp.arange(hn2.shape[0])]
        return x + moe.reshape(b, s, h)
    x = x + _L0_xattn_ref(_layernorm(x, axis=-1), ctx_1024, L0_xattn_ln_g, L0_xattn_ln_b, L0_xattn_cln_g, L0_xattn_cln_b, L0_xattn_Wq, L0_xattn_Wkv, L0_xattn_Wo, L0_xattn_Wff1, L0_xattn_Wff2)
    x = x + _L0_ffn_ref(_layernorm(x, axis=-1), L0_ffn_ln1_g, L0_ffn_ln1_b, L0_ffn_ln2_g, L0_ffn_ln2_b, L0_ffn_wq, L0_ffn_bq, L0_ffn_wk, L0_ffn_bk, L0_ffn_wv, L0_ffn_bv, L0_ffn_wo, L0_ffn_bo, L0_ffn_gate_w, L0_ffn_gate_b, L0_ffn_w1, L0_ffn_b1, L0_ffn_w2, L0_ffn_b2)
    return x

_drawn_inputs = setup_inputs


def setup_inputs(seed=0):
    import zlib

    import numpy as np

    out = dict(_drawn_inputs(seed))
    spreads = {'L0_xattn_ln_g': (1.0, 0.2),
     'L0_xattn_ln_b': (0.0, 0.1),
     'L0_xattn_cln_g': (1.0, 0.2),
     'L0_xattn_cln_b': (0.0, 0.1),
     'L0_ffn_ln1_g': (1.0, 0.6),
     'L0_ffn_ln1_b': (0.0, 0.8),
     'L0_ffn_ln2_g': (1.0, 0.2),
     'L0_ffn_ln2_b': (0.0, 0.465),
     'L0_ffn_bq': (0.0, 0.8),
     'L0_ffn_bk': (0.0, 0.8),
     'L0_ffn_bv': (0.0, 0.523),
     'L0_ffn_bo': (0.0, 0.1),
     'L0_ffn_gate_b': (0.0, 0.1),
     'L0_ffn_b1': (0.0, 0.617),
     'L0_ffn_b2': (0.0, 0.1)}
    factors = {'L0_ffn_wq': 8.0, 'L0_ffn_wk': 8.0, 'L0_ffn_wv': 4.254, 'L0_ffn_wo': 3.195}
    for name, (base, spread) in spreads.items():
        noise = np.random.default_rng([zlib.crc32(name.encode()), seed]).standard_normal(out[name].shape)
        drawn = base * np.exp(spread * noise) if base else spread * noise
        out[name] = jnp.asarray(drawn.astype(out[name].dtype))
    for name, factor in factors.items():
        out[name] = (out[name] * factor).astype(out[name].dtype)
    return out
```

```python
from contextlib import ExitStack

import concourse.bass as bass
from concourse import mybir
from concourse.alu_op_type import AluOpType as ALU

F32 = mybir.dt.float32
I32 = mybir.dt.int32
ACT = mybir.ActivationFunctionType
AX_X = mybir.AxisListType.X

P = 128
SEQ = 64
PER_TILE = P // SEQ
TILES = 4
GT = TILES * P
GB = GT // SEQ
HEADS = 16
HP = HEADS // 2
D1 = 64
D2 = P // HEADS
FF = 512
FC = FF // P
EXPERTS = 8
BLOCK = 256
BA = BLOCK // P
EPS = 1e-5
RSQRT_GUESS = float(0x5F3759DF)
SCALE1 = float(D1) ** -0.5
SCALE2 = float(D2) ** -0.5
LN_G, LN_B, CLN_G, CLN_B, LN1_G, LN1_B, LN2_G, LN2_B, BQ, BK = range(10)
EW1, EW2, EB1, EB2, EN = 0, FF, FF + FC * P, FF + FC * P + FC, FF + FC * P + FC + 1


def psum_uses(attn1, attn2, prepare):
    uses = []
    if attn1:
        uses += ["K", "V"]
    if attn2:
        uses += ["Y"]
    if attn1:
        uses += [f"Q{h}" for h in range(4)]
    if attn2:
        uses += ["H"]
    if attn1:
        uses += [f"Q{h}" for h in range(4, HP)]
    if attn2:
        uses += ["q2", "k2", "v2a", "v2b"]
    for p in range(TILES):
        if attn1 and p:
            uses += [f"o1a{p - 1}", f"o1b{p - 1}"]
        if attn1:
            uses += [f"fh{p}", f"fg{p}"]
        if attn2 and p:
            uses += [f"o2{p - 1}"]
    if attn1:
        uses += [f"o1a{TILES - 1}", f"o1b{TILES - 1}"]
    if prepare:
        uses += ["X", "C"]
    if attn2:
        uses += [f"o2{TILES - 1}", "O", "P"]
    if attn1:
        uses += ["W"]
    if attn2:
        uses += ["G", "L"]
    return uses


MIDDLE_VECTOR_STEPS = 89


class Step:

    def __init__(self, g, attn1, attn2, prepare, before):
        self.g, self.attn1, self.attn2, self.prepare = g, attn1, attn2, prepare
        self.uses = psum_uses(attn1, attn2, prepare)
        self.used = [before(0), before(1)]

    def bank(self, name):
        return self.uses.index(name) % 2

    def full(self, name):
        k = self.uses.index(name)
        return self.used[k % 2] + k // 2 + 1

    def item1(self, p):
        return TILES * self.g + p

    def item2(self, p):
        return TILES * (self.g - 1) + p


def wait(engine, semaphore, value):
    if isinstance(value, int) and value <= 0:
        return
    engine.wait_ge(semaphore, value)


def build(nc, x, ctx_in, wq1, wk1, wv1, wo1, wff1, wff2, wq2, wk2, wv2, wo2, vectors, bv, bo, gate_w,
          gate_b, experts, out):
    tokens = x.shape[0]
    groups = tokens // GT
    tiles = tokens // P
    blocks = tokens // BLOCK + EXPERTS - 1
    sorted_rows = blocks * BLOCK

    sorted_in = nc.dram_tensor("sorted_in", [sorted_rows, P], F32, kind="Internal").ap()
    sorted_out = nc.dram_tensor("sorted_out", [sorted_rows, P], F32, kind="Internal").ap()

    es = ExitStack()
    with es:
        def sb(name, shape, dt=F32):
            return es.enter_context(nc.sbuf_tensor(name, shape, dt))

        def ps(name, shape):
            return es.enter_context(nc.psum_tensor(name, shape, F32))

        def sem(name):
            return es.enter_context(nc.semaphore(name))

        wq1_s = sb("wq1_s", [P, HEADS * D1])
        wk1_s = sb("wk1_s", [P, 2, D1])
        wv1_s = sb("wv1_s", [P, D1])
        wo1_s = sb("wo1_s", [P, HP, P])
        wff1_s = sb("wff1_s", [P, 2 * FF])
        wff2_s = sb("wff2_s", [P, FC, P])
        wq2_s = sb("wq2_s", [P, P])
        wk2_s = sb("wk2_s", [P, P])
        wv2_s = sb("wv2_s", [P, P])
        wo2_s = sb("wo2_s", [P, P])
        vec = sb("vec", [P, 10])
        bv_s = sb("bv_s", [P, P])
        bo_s = sb("bo_s", [P, P])
        gw_s = sb("gw_s", [P, EXPERTS])
        gb_s = sb("gb_s", [P, EXPERTS])
        ident = sb("ident", [P, P])
        head_mask = sb("head_mask", [P, HEADS])
        below = sb("below", [P, P])
        ones = sb("ones", [P, 256])
        first_wins = sb("first_wins", [P, EXPERTS])
        starts = sb("starts", [P, blocks])
        starts_i = sb("starts_i", [P, blocks], I32)
        first_wins_i = sb("first_wins_i", [P, EXPERTS], I32)

        x_s = sb("x_s", [P, tiles, P])
        c_s = sb("c_s", [P, tiles, P])
        total = sb("total", [P, tiles, P])
        h2_all = sb("h2_all", [P, tiles, P])
        logits = sb("logits", [P, tiles, EXPERTS])

        xh = sb("xh", [P, TILES, P])
        ch = sb("ch", [P, TILES, P])
        xnT = sb("xnT", [P, GT])
        cnT = sb("cnT", [P, GT])
        kblock = sb("kblock", [P, GB, 2, SEQ])
        vblock = sb("vblock", [P, GB, 2, D1])
        qT = sb("qT", [P, HP, GT])
        oT = sb("oT", [P, HP, GT])
        tanh_g = sb("tanh_g", [P, GT])
        ffT = sb("ffT", [P, FC, GT])
        prob1 = sb("prob1", [P, HEADS, SEQ])
        prob2 = sb("prob2", [P, HEADS, SEQ])
        pT1 = sb("pT1", [P, HP, P])
        pT2 = sb("pT2", [P, HP, P])
        yT = sb("yT", [P, GT])
        x1 = sb("x1", [P, TILES, P])
        z = sb("z", [P, TILES, P])
        hn = sb("hn", [P, TILES, P])
        hnT = sb("hnT", [P, GT])
        q2T = sb("q2T", [P, GT])
        k2T = sb("k2T", [P, GT])
        v2block = sb("v2block", [P, GB, HP, 2, D2])
        kspread = sb("kspread", [P, 2, PER_TILE, HEADS, SEQ])
        o2 = sb("o2", [P, TILES, P])
        o2T = sb("o2T", [P, GT])
        h2 = sb("h2", [P, TILES, P])
        h2T = hnT
        max1 = sb("max1", [P, HEADS])
        max2 = sb("max2", [P, HEADS])
        sum1 = sb("sum1", [P, HEADS])
        sum2 = sb("sum2", [P, HEADS])
        inv1 = sb("inv1", [P, HEADS])
        inv2 = sb("inv2", [P, HEADS])
        chosen = sb("chosen", [P, tiles, EXPERTS])
        lmax = sb("lmax", [P, tiles])
        position = sb("position", [P, tiles])
        position_i = sb("position_i", [P, tiles], I32)
        count_et = sb("count_et", [P, EXPERTS, tiles])
        upto = sb("upto", [P, EXPERTS, tiles])
        spots = sb("spots", [P, tiles, EXPERTS])
        rows_of = sb("rows_of", [P, EXPERTS])
        padded = sb("padded", [P, EXPERTS])
        padded_end = sb("padded_end", [P, EXPERTS])
        shift = sb("shift", [P, EXPERTS])
        compare = sb("compare", [P, EXPERTS, blocks])
        compare_b = sb("compare_b", [P, blocks, EXPERTS])
        block_expert = sb("block_expert", [P, blocks])
        block_expert_i = sb("block_expert_i", [P, blocks], I32)
        stat = sb("stat", [P, 2 * TILES, 6])
        carrier = sb("carrier", [P, 1])
        mv = sb("mv", [P, 2 * TILES, 2])
        var = sb("var", [P, 2 * TILES])
        half_var = sb("half_var", [P, 2 * TILES])
        square = sb("square", [P, 2 * TILES])
        rstd = sb("rstd", [P, 2 * TILES])

        oT_flat = oT[:].rearrange("p h t -> p (h t)")
        expert_w = [oT_flat[:, i * EN:(i + 1) * EN] for i in range(2)]
        qT_flat = qT[:].rearrange("p h t -> p (h t)")

        def from_q(at, shape):
            n = shape[0] * (shape[1] if len(shape) > 1 else 1)
            piece = qT_flat[:, at:at + n]
            return piece.rearrange("p (a b) -> p a b", a=shape[0]) if len(shape) > 1 else piece

        block_rows = [from_q(i * BLOCK, [BA, P]) for i in range(2)]
        blockT = [from_q((2 + i) * BLOCK, [BLOCK]) for i in range(2)]
        mid = [from_q((4 + i * FC) * BLOCK, [FC, BLOCK]) for i in range(2)]
        y_T = [from_q((12 + i) * BLOCK, [BLOCK]) for i in range(2)]
        y_rows = [from_q((14 + i) * BLOCK, [BA, P]) for i in range(2)]
        expert_rows = x_s

        score1 = ps("score1", [P, HEADS, SEQ])
        score2 = ps("score2", [P, HEADS, SEQ])
        transposed = ps("transposed", [P, HP, P])
        shared = [ps(f"shared{i}", [P, GT]) for i in range(2)]

        weights_in = sem("weights_in")
        rows0_in = sem("rows0_in")
        rows_in = sem("rows_in")
        scratch_clear = sem("scratch_clear")
        const_step = sem("const_step")
        const_ready = sem("const_ready")
        half_w = sem("half_w")
        dve_done = sem("dve_done")
        rows_normed = sem("rows_normed")
        bank_full = [sem(f"bank_full{i}") for i in range(2)]
        bank_free = [sem(f"bank_free{i}") for i in range(2)]
        score1_full = sem("score1_full")
        score1_free = sem("score1_free")
        exp1_done = sem("exp1_done")
        inv1_ready = sem("inv1_ready")
        prob1_ready = sem("prob1_ready")
        score2_full = sem("score2_full")
        score2_free = sem("score2_free")
        exp2_done = sem("exp2_done")
        inv2_ready = sem("inv2_ready")
        prob2_ready = sem("prob2_ready")
        tr_full = sem("tr_full")
        tr_free = sem("tr_free")
        tanh_done = sem("tanh_done")
        hn_ready = sem("hn_ready")
        spread_ready = sem("spread_ready")
        h2_ready = sem("h2_ready")
        h2_kept = sem("h2_kept")
        chosen_ready = sem("chosen_ready")
        counted = sem("counted")
        positions_ready = sem("positions_ready")
        block_expert_ready = sem("block_expert_ready")
        scattered = sem("scattered")
        expert_in = [sem(f"expert_in{i}") for i in range(2)]
        block_in = [sem(f"block_in{i}") for i in range(2)]
        block_turned = sem("block_turned")
        block_T = sem("block_T")
        mid_full = sem("mid_full")
        mid_ready = sem("mid_ready")
        y_full = sem("y_full")
        yT_ready = sem("yT_ready")
        y_turned = sem("y_turned")
        y_rows_ready = sem("y_rows_ready")
        block_stored = [sem(f"block_stored{i}") for i in range(2)]
        gathered = [sem(f"gathered{i}") for i in range(groups)]
        group_done = sem("group_done")
        out_stored = sem("out_stored")

        FIRST = dict(attn1=True, attn2=False, prepare=True)
        MID = dict(attn1=True, attn2=True, prepare=True)
        LAST = dict(attn1=True, attn2=True, prepare=False)
        DRAIN = dict(attn1=False, attn2=True, prepare=False)

        def in_bank(kind, b):
            n = len(psum_uses(**kind))
            return (n + 1 - b) // 2

        def first_step():
            return Step(0, before=lambda b: 1, **FIRST)

        def middle_step(g):
            return Step(g, before=lambda b: 1 + in_bank(FIRST, b) + (g - 1) * in_bank(MID, b), **MID)

        def last_step():
            g = groups - 1
            return Step(g, before=lambda b: 1 + in_bank(FIRST, b) + (g - 1) * in_bank(MID, b), **LAST)

        def drain_step():
            return Step(groups, before=lambda b: 1 + in_bank(FIRST, b) + (groups - 2) * in_bank(MID, b)
                        + in_bank(LAST, b), **DRAIN)

        def wait_read(engine, s, name):
            engine.wait_ge(bank_free[s.bank(name)], s.full(name))

        def run_pipeline(engine, body):
            body(first_step())
            with engine.Fori(1, groups - 1) as g:
                body(middle_step(g))
            body(last_step())
            body(drain_step())

        def transposes_before(s):
            if isinstance(s.g, int) and s.g == 0:
                return 0
            return TILES + (s.g - 1) * 2 * TILES

        tr_order = {}
        for kind, (a1, a2) in (("first", (True, False)), ("mid", (True, True)), ("drain", (False, True))):
            order = []
            for p in range(TILES):
                if a2 and p:
                    order.append(("2", p - 1))
                if a1:
                    order.append(("1", p))
            if a2:
                order.append(("2", TILES - 1))
            tr_order[(a1, a2)] = order

        def tr_index(s, which, p):
            return transposes_before(s) + tr_order[(s.attn1, s.attn2)].index((which, p))

        tile_ranks = score1[:].rearrange("p h j -> p (h j)")[:, 0:tiles * EXPERTS]
        tile_counts = score1[:].rearrange("p h j -> p (h j)")[:, GT:GT + tiles * EXPERTS]

        def mid_bank(slot, c):
            return (score1, score2)[slot][:].rearrange("p h j -> p (h j)")[:, c * BLOCK:(c + 1) * BLOCK]

        block = es.enter_context(nc.Block())

        WEIGHTS_IN = 16 * 16
        CLEARS = -(-sorted_rows // (tiles * P))

        def for_blocks(engine, run):
            run(0, 0)
            run(1, 1)
            with engine.Fori(1, blocks // 2) as i:
                run(2 * i, 0)
                run(2 * i + 1, 1)
            if blocks % 2:
                run(blocks - 1, 0)

        def nth_of(s, slot):
            return (s - slot) // 2 + 1

        @block.sync
        def _(sp):
            xv = x.rearrange("(t p) d -> p t d", p=P)
            cv = ctx_in.rearrange("(t p) d -> p t d", p=P)
            sp.dma_start(x_s[:, 0:TILES, :], xv[:, 0:TILES, :]).then_inc(rows0_in, 16)
            sp.dma_start(c_s[:, 0:TILES, :], cv[:, 0:TILES, :]).then_inc(rows0_in, 16)
            sp.dma_start(vec[:], vectors).then_inc(weights_in, 16)
            for half in range(2):
                sp.dma_start(wk1_s[:, half, :], wk1).then_inc(weights_in, 16)
            sp.dma_start(wv1_s[:], wv1).then_inc(weights_in, 16)
            sp.dma_start(wq1_s[:], wq1).then_inc(weights_in, 16)
            sp.dma_start(wff1_s[:], wff1).then_inc(weights_in, 16)
            sp.dma_start(wff2_s[:], wff2.rearrange("(c p) n -> p c n", p=P)).then_inc(weights_in, 16)
            sp.dma_start(wo1_s[:], wo1.rearrange("(c p) n -> p c n", p=P)).then_inc(weights_in, 16)
            for to, of in ((wq2_s, wq2), (wk2_s, wk2), (wv2_s, wv2), (wo2_s, wo2), (gw_s, gate_w)):
                sp.dma_start(to[:], of).then_inc(weights_in, 16)
            for to, of in ((bv_s, bv), (bo_s, bo), (gb_s, gate_b)):
                sp.dma_start(to[:], of.partition_broadcast(P)).then_inc(weights_in, 16)
            sp.dma_start(x_s[:, TILES:, :], xv[:, TILES:, :]).then_inc(rows_in, 16)
            sp.dma_start(c_s[:, TILES:, :], cv[:, TILES:, :]).then_inc(rows_in, 16)
            sp.wait_ge(const_ready, 1)
            per = sorted_rows // P * P
            flat = sorted_in.rearrange("(p r) d -> p (r d)", p=P)
            zero = h2_all[:].rearrange("p t d -> p (t d)")
            for at in range(0, per, tiles * P):
                n = min(tiles * P, per - at)
                sp.dma_start(flat[:, at:at + n], zero[:, 0:n]).then_inc(scratch_clear, 16)

            def load_block(s, slot):
                wait(sp, yT_ready, s - 1)
                e = sp.value_load(block_expert_i[0:1, bass.ds(s, 1)], min_val=0, max_val=EXPERTS - 1)
                sp.dma_start(expert_w[slot], experts[bass.ds(e, 1)].rearrange("e p n -> (e p) n")).then_inc(
                    expert_in[slot], 16)
                sp.dma_start(block_rows[slot], sorted_in[bass.ds(s * BLOCK, BLOCK), :].rearrange(
                    "(p a) d -> p a d", p=P)).then_inc(block_in[slot], 16)

            sp.wait_ge(block_expert_ready, 1)
            sp.wait_ge(scattered, 16 * tiles)
            for_blocks(sp, load_block)
            ov = out.rearrange("(t p) d -> p t d", p=P)
            for g in range(groups):
                sp.wait_ge(group_done, g + 1)
                sp.dma_start(ov[:, g * TILES:(g + 1) * TILES, :], total[:, g * TILES:(g + 1) * TILES, :]).then_inc(
                    out_stored, 16)
            sp.wait_ge(out_stored, 16 * groups)

        @block.gpsimd
        def _(pool):
            steps = [0]

            def step(ins):
                steps[0] += 1
                ins.then_inc(const_step, 1)
                pool.wait_ge(const_step, steps[0])

            nc.gpsimd.memset(ident[:], 0.0)
            nc.gpsimd.memset(head_mask[:], 1.0)
            nc.gpsimd.memset(kblock[:], 0.0)
            nc.gpsimd.memset(vblock[:], 0.0)
            nc.gpsimd.memset(v2block[:], 0.0)
            nc.gpsimd.memset(ones[:], 1.0)
            nc.gpsimd.memset(h2_all[:], 0.0)
            step(nc.gpsimd.memset(below[:], 1.0))
            step(nc.gpsimd.affine_select(out=ident[:], in_=ident[:], compare_op=ALU.not_equal, fill=1.0,
                                         base=0, pattern=[[-1, P]], channel_multiplier=1))
            step(nc.gpsimd.affine_select(out=head_mask[:], in_=head_mask[:], compare_op=ALU.is_ge, fill=0.0,
                                         base=0, pattern=[[-D2, HEADS]], channel_multiplier=1))
            step(nc.gpsimd.affine_select(out=head_mask[:], in_=head_mask[:], compare_op=ALU.is_ge, fill=0.0,
                                         base=D2 - 1, pattern=[[D2, HEADS]], channel_multiplier=-1))
            step(nc.gpsimd.affine_select(out=below[:], in_=below[:], compare_op=ALU.is_gt, fill=0.0,
                                         base=0, pattern=[[1, P]], channel_multiplier=-1))
            nc.gpsimd.iota(first_wins_i[:], pattern=[[-1, EXPERTS]], base=EXPERTS, channel_multiplier=0)
            step(nc.gpsimd.iota(starts_i[:], pattern=[[BLOCK, blocks]], base=0, channel_multiplier=0))
            nc.gpsimd.tensor_copy(first_wins[:], first_wins_i[:])
            nc.gpsimd.tensor_copy(starts[:], starts_i[:]).then_inc(const_ready, 1)

            def spread(s, p):
                for b in range(PER_TILE):
                    at = (PER_TILE * p + b) * SEQ
                    ins = nc.gpsimd.tensor_tensor(
                        kspread[:, p % 2, b], k2T[:, None, at:at + SEQ].to_broadcast([P, HEADS, SEQ]),
                        head_mask[:, :, None].to_broadcast([P, HEADS, SEQ]), ALU.mult)
                ins.then_inc(spread_ready, 1)

            def normalise(prob, inv, inv_ready, count, ready):
                pool.wait_ge(inv_ready, count + 1)
                nc.gpsimd.tensor_tensor(prob[:], prob[:], inv[:, :, None].to_broadcast([P, HEADS, SEQ]),
                                        ALU.mult).then_inc(ready, 1)

            def body(s):
                if s.attn2:
                    wait_read(pool, s, "k2")
                    spread(s, 0)
                for p in range(TILES):
                    if s.attn2 and p:
                        normalise(prob2, inv2, inv2_ready, s.item2(p - 1), prob2_ready)
                    if s.attn1:
                        normalise(prob1, inv1, inv1_ready, s.item1(p), prob1_ready)
                    if s.attn2 and p + 1 < TILES:
                        if p:
                            pool.wait_ge(score2_full, s.item2(p - 1) + 1)
                        spread(s, p + 1)
                if s.attn2:
                    normalise(prob2, inv2, inv2_ready, s.item2(TILES - 1), prob2_ready)
                    pool.wait_ge(scratch_clear, 16 * CLEARS)
                    pool.wait_ge(h2_ready, s.g)
                    at = TILES * (s.g - 1)
                    nc.gpsimd.tensor_copy(h2_all[:, bass.ds(at, TILES), :], h2[:]).then_inc(h2_kept, 1)

            run_pipeline(pool, body)
            pool.wait_ge(positions_ready, 1)
            pool.wait_ge(h2_kept, groups)
            for t in range(tiles):
                nc.gpsimd.indirect_dma_start(
                    out=sorted_in, out_offset=bass.IndirectOffsetOnAxis(ap=position_i[:, t:t + 1], axis=0),
                    in_=h2_all[:, t, :], in_offset=None).then_inc(scattered, 16)
            pool.wait_ge(block_stored[0], 16 * ((blocks + 1) // 2))
            pool.wait_ge(block_stored[1], 16 * (blocks // 2))
            for t in range(tiles):
                nc.gpsimd.indirect_dma_start(
                    out=expert_rows[:, t, :], out_offset=None, in_=sorted_out,
                    in_offset=bass.IndirectOffsetOnAxis(ap=position_i[:, t:t + 1], axis=0)).then_inc(
                        gathered[t // TILES], 16)

        @block.scalar
        def _(act):
            def take(s, name):
                act.wait_ge(bank_full[s.bank(name)], s.full(name))
                return shared[s.bank(name)]

            def affine(to, bank, gain, bias):
                return nc.scalar.activation(to[:], bank[:], ACT.Identity, bias=vec[:, bias:bias + 1],
                                            scale=vec[:, gain:gain + 1])

            def free(s, name, ins):
                ins.then_inc(bank_free[s.bank(name)], 1)

            def copy_out(which, to, s, p):
                act.wait_ge(tr_full, tr_index(s, which, p) + 1)
                nc.scalar.copy(to[:, 0:HP // 2, :], transposed[:, 0:HP // 2, :])
                nc.scalar.copy(to[:, HP // 2:, :], transposed[:, HP // 2:, :]).then_inc(tr_free, 1)

            def out1(s, p):
                for b in range(PER_TILE):
                    bank = take(s, f"o1{'ab'[b]}{p}")
                    at = p * P + b * SEQ
                    free(s, f"o1{'ab'[b]}{p}",
                         nc.scalar.copy(oT[:, :, at:at + SEQ], bank[:].rearrange("p (h i) -> p h i", h=HP)))

            def out2(s, p):
                bank = take(s, f"o2{p}")[:, 0:PER_TILE * P].rearrange("p (h b c) -> p h b c", h=HP, b=PER_TILE)
                to = o2[:, p, :].rearrange("p (h c) -> p h c", h=HP)
                nc.scalar.copy(to[0:SEQ], bank[0:SEQ, :, 0, :])
                free(s, f"o2{p}", nc.scalar.copy(to[SEQ:P], bank[SEQ:P, :, 1, :]))

            def prep(banks, wait_full):
                for bank, to, gain, bias in ((0, xnT, LN_G, LN_B), (1, cnT, CLN_G, CLN_B)):
                    wait_full(bank)
                    b = banks[bank]
                    affine(to, shared[b], gain, bias).then_inc(bank_free[b], 1)

            act.wait_ge(weights_in, WEIGHTS_IN)
            act.wait_ge(const_ready, 1)
            prep([0, 1], lambda b: act.wait_ge(bank_full[b], 1))

            def body(s):
                if s.attn1:
                    bank = take(s, "K")[:].rearrange("p (b j) -> p b j", b=GB)
                    nc.scalar.copy(kblock[0:SEQ, :, 0, :], bank[0:SEQ])
                    free(s, "K", nc.scalar.copy(kblock[SEQ:P, :, 1, :], bank[SEQ:P]))
                    bank = take(s, "V")[:].rearrange("p (b j) -> p b j", b=GB)
                    nc.scalar.copy(vblock[0:SEQ, :, 0, :], bank[0:SEQ])
                    free(s, "V", nc.scalar.copy(vblock[SEQ:P, :, 1, :], bank[SEQ:P]))
                    for h in range(HP // 2):
                        free(s, f"Q{h}", nc.scalar.copy(qT[:, h, :], take(s, f"Q{h}")[:]))
                if s.attn2:
                    free(s, "H", affine(hnT, take(s, "H"), LN1_G, LN1_B))
                if s.attn1:
                    for h in range(HP // 2, HP):
                        free(s, f"Q{h}", nc.scalar.copy(qT[:, h, :], take(s, f"Q{h}")[:]))
                if s.attn2:
                    for name, to, bias in (("q2", q2T, BQ), ("k2", k2T, BK)):
                        bank = take(s, name)
                        free(s, name, nc.scalar.activation(to[:], bank[:], ACT.Identity, bias=vec[:, bias:bias + 1]))
                for p in range(TILES):
                    if s.attn1 and p:
                        out1(s, p - 1)
                    if s.attn1:
                        act.wait_ge(score1_free, s.item1(p) + 1)
                        nc.scalar.activation(prob1[:], prob1[:], ACT.Exp, scale=SCALE1).then_inc(exp1_done, 1)
                    if s.attn2 and p:
                        copy_out("2", pT2, s, p - 1)
                    if s.attn1:
                        bank = take(s, f"fg{p}")
                        nc.scalar.activation(tanh_g[:], bank[:], ACT.Tanh, scale=0.5).then_inc(tanh_done, 1)
                    if s.attn2 and p:
                        out2(s, p - 1)
                    if s.attn2:
                        act.wait_ge(score2_free, s.item2(p) + 1)
                        nc.scalar.activation(prob2[:], prob2[:], ACT.Exp, scale=SCALE2).then_inc(exp2_done, 1)
                    if s.attn1:
                        copy_out("1", pT1, s, p)
                if s.attn1:
                    out1(s, TILES - 1)
                if s.attn2:
                    copy_out("2", pT2, s, TILES - 1)
                if s.prepare:
                    prep([s.bank("X"), s.bank("C")], lambda b: take(s, "XC"[b]))
                if s.attn2:
                    out2(s, TILES - 1)
                    free(s, "O", nc.scalar.copy(o2T[:], take(s, "O")[:]))
                if s.attn1:
                    free(s, "W", nc.scalar.copy(yT[:], take(s, "W")[:]))
                if s.attn2:
                    free(s, "G", affine(h2T, take(s, "G"), LN2_G, LN2_B))

            run_pipeline(act, body)

            def experts_out(s, slot):
                act.wait_ge(block_turned, s + 1)
                nc.scalar.activation(blockT[slot][:], shared[0][:, 0:BLOCK], ACT.Identity,
                                     bias=vec[:, LN2_B:LN2_B + 1], scale=vec[:, LN2_G:LN2_G + 1]).then_inc(block_T, 1)
                if not (isinstance(s, int) and s == 0):
                    store(s - 1, 1 - slot)

            def store(s, slot):
                act.wait_ge(y_turned, s + 1)
                if not (isinstance(s, int) and s < 2):
                    act.wait_ge(block_stored[slot], 16 * (nth_of(s, slot) - 1))
                nc.scalar.copy(y_rows[slot].rearrange("p a d -> p (a d)"),
                               transposed[:].rearrange("p h c -> p (h c)")[:, 0:BLOCK]).then_inc(y_rows_ready, 1)
                act.wait_ge(y_rows_ready, s + 1)
                act.dma_start(sorted_out[bass.ds(s * BLOCK, BLOCK), :].rearrange("(p a) d -> p a d", p=P),
                              y_rows[slot]).then_inc(block_stored[slot], 16)

            for_blocks(act, experts_out)
            store(blocks - 1, (blocks - 1) % 2)

        @block.vector
        def _(dve):
            count = {"base": 0, "n": 0}

            def step(ins):
                count["n"] += 1
                ins.then_inc(dve_done, 1)
                dve.wait_ge(dve_done, count["base"] + count["n"])

            def norm(*pairs):
                n = TILES * len(pairs)
                for t in range(n):
                    last = nc.vector.bn_stats(stat[:, t, :], pairs[t // TILES][0][:, t % TILES, :])
                step(last)
                nc.vector.memset(carrier[:], 0.0)
                for t in range(n):
                    last = nc.vector.bn_aggr(mv[:, t, :], stat[:, t, :])
                step(last)
                v, half, y, t2 = var[:, 0:n], half_var[:, 0:n], rstd[:, 0:n], square[:, 0:n]
                step(nc.vector.tensor_scalar(v, mv[:, 0:n, 1], EPS, None, ALU.add))
                nc.vector.tensor_scalar(half, v, -0.5, None, ALU.mult)
                step(nc.vector.tensor_scalar(t2.bitcast(I32), v.bitcast(I32), 1, None, ALU.arith_shift_right))
                step(nc.vector.tensor_scalar(y.bitcast(I32), t2.bitcast(I32), -1.0, RSQRT_GUESS, ALU.mult, ALU.add))
                for _ in range(3):
                    step(nc.vector.tensor_tensor(t2, y, y, ALU.mult))
                    step(nc.vector.tensor_tensor(t2, t2, half, ALU.mult))
                    step(nc.vector.scalar_tensor_tensor(out=y, in0=t2, scalar=1.5, in1=y, op0=ALU.add, op1=ALU.mult))
                for t in range(n):
                    src, dst = pairs[t // TILES]
                    last = nc.vector.tensor_scalar(dst[:, t % TILES, :], src[:, t % TILES, :], mv[:, t, 0:1],
                                                   y[:, t:t + 1], ALU.subtract, ALU.mult)
                return last

            def less_max(score, mx, prob, free_sem):
                step(nc.vector.reduce_max(mx[:], score[:], AX_X))
                nc.vector.tensor_tensor(prob[:], score[:], mx[:, :, None].to_broadcast([P, HEADS, SEQ]),
                                        ALU.subtract).then_inc(free_sem, 1)

            def invert_sum(prob, sm, inv, ready):
                step(nc.vector.reduce_sum(sm[:], prob[:], AX_X))
                nc.vector.reciprocal(inv[:], sm[:]).then_inc(ready, 1)

            def group_rows(rows, g):
                return rows[:, bass.ds(g * TILES, TILES), :] if not isinstance(g, int) else \
                    rows[:, g * TILES:(g + 1) * TILES, :]

            dve.wait_ge(rows0_in, 32)
            step(norm((x_s[:, 0:TILES, :], xh), (c_s[:, 0:TILES, :], ch)))
            norm((xh, xh)).then_inc(rows_normed, 1)
            dve.wait_ge(rows_normed, 1)
            dve.wait_ge(weights_in, WEIGHTS_IN)
            nc.vector.tensor_scalar(wff2_s[:], wff2_s[:], 0.5, None, ALU.mult).then_inc(half_w, 1)
            dve.wait_ge(rows_in, 32)
            dve.wait_ge(const_ready, 1)

            def body(s):
                if s.attn2:
                    g = s.g - 1
                    dve.wait_ge(bank_full[s.bank("Y")], s.full("Y"))
                    ins = nc.vector.tensor_tensor(x1[:], group_rows(x_s, g),
                                                  shared[s.bank("Y")][:].rearrange("p (t d) -> p t d", t=TILES),
                                                  ALU.add)
                    ins.then_inc(bank_free[s.bank("Y")], 1)
                    wait_read(dve, s, "Y")
                    step(norm((x1, z)))
                    norm((z, hn)).then_inc(hn_ready, 1)
                    dve.wait_ge(hn_ready, s.g)
                    step(nc.vector.tensor_tensor(z[:], z[:], bo_s[:, None, :].to_broadcast([P, TILES, P]), ALU.add))
                    for half, name in enumerate(("v2a", "v2b")):
                        dve.wait_ge(bank_full[s.bank(name)], s.full(name))
                        bank = shared[s.bank(name)][:].rearrange("p (b h c d) -> p b h c d", b=GB // 2, h=HP, c=2)
                        bias = bv_s[:].rearrange("p (h c d) -> p h c d", h=HP, c=2)
                        to = v2block[:, half * GB // 2:(half + 1) * GB // 2]
                        for c in range(2):
                            rows = slice(c * SEQ, (c + 1) * SEQ)
                            for b in range(GB // 2):
                                last = nc.vector.tensor_tensor(to[rows, b, :, c, :], bank[rows, b, :, c, :],
                                                               bias[rows, :, c, :], ALU.add)
                        last.then_inc(bank_free[s.bank(name)], 1)
                for p in range(TILES):
                    if s.attn2 and p:
                        dve.wait_ge(exp2_done, s.item2(p - 1) + 1)
                        invert_sum(prob2, sum2, inv2, inv2_ready)
                    if s.attn1:
                        dve.wait_ge(score1_full, s.item1(p) + 1)
                        less_max(score1, max1, prob1, score1_free)
                        dve.wait_ge(exp1_done, s.item1(p) + 1)
                        invert_sum(prob1, sum1, inv1, inv1_ready)
                        dve.wait_ge(tanh_done, s.item1(p) + 1)
                        fg, fh = s.bank(f"fg{p}"), s.bank(f"fh{p}")
                        ins = nc.vector.scalar_tensor_tensor(out=tanh_g[:], in0=tanh_g[:], scalar=1.0,
                                                             in1=shared[fg][:], op0=ALU.add, op1=ALU.mult)
                        ins.then_inc(bank_free[fg], 1)
                        wait_read(dve, s, f"fg{p}")
                        ins = nc.vector.tensor_tensor(ffT[:, p, :], tanh_g[:], shared[fh][:], ALU.mult)
                        ins.then_inc(bank_free[fh], 1)
                    if s.attn2:
                        dve.wait_ge(score2_full, s.item2(p) + 1)
                        less_max(score2, max2, prob2, score2_free)
                    if s.prepare and p == 0:
                        step(norm((group_rows(x_s, s.g + 1), xh), (group_rows(c_s, s.g + 1), ch)))
                    if s.prepare and p == 1:
                        norm((xh, xh)).then_inc(rows_normed, 1)
                        dve.wait_ge(rows_normed, s.g + 2)
                if s.attn2:
                    g = s.g - 1
                    dve.wait_ge(exp2_done, s.item2(TILES - 1) + 1)
                    invert_sum(prob2, sum2, inv2, inv2_ready)
                    dve.wait_ge(bank_full[s.bank("P")], s.full("P"))
                    ins = nc.vector.tensor_tensor(z[:], z[:], shared[s.bank("P")][:].rearrange(
                        "p (t d) -> p t d", t=TILES), ALU.add)
                    ins.then_inc(bank_free[s.bank("P")], 1)
                    wait_read(dve, s, "P")
                    wait(dve, h2_kept, s.g - 1)
                    norm((z, h2)).then_inc(h2_ready, 1)
                    dve.wait_ge(h2_ready, s.g)
                    nc.vector.tensor_tensor(group_rows(total, g), x1[:], z[:], ALU.add)
                    dve.wait_ge(bank_full[s.bank("L")], s.full("L"))
                    nc.vector.tensor_tensor(
                        group_rows(logits, g),
                        shared[s.bank("L")][:, 0:TILES * EXPERTS].rearrange("p (t e) -> p t e", t=TILES),
                        gb_s[:, None, :].to_broadcast([P, TILES, EXPERTS]), ALU.add).then_inc(
                            bank_free[s.bank("L")], 1)

            body(first_step())
            first_end = count["n"]
            per_middle = MIDDLE_VECTOR_STEPS
            with dve.Fori(1, groups - 1) as g:
                count["base"], count["n"] = (g - 1) * per_middle + first_end, 0
                body(middle_step(g))
                assert count["n"] == per_middle, f"MIDDLE_VECTOR_STEPS is {count['n']}"
            count["base"], count["n"] = 0, first_end + (groups - 2) * per_middle
            body(last_step())
            body(drain_step())

            def over_rows(v):
                return v[:, :, None].to_broadcast([P, tiles, EXPERTS])

            step(nc.vector.memset(lmax[:], 0.0))
            step(nc.vector.reduce_max(lmax[:], logits[:], AX_X))
            step(nc.vector.tensor_tensor(chosen[:], logits[:], over_rows(lmax), ALU.is_equal))
            step(nc.vector.tensor_tensor(chosen[:], chosen[:],
                                         first_wins[:, None, :].to_broadcast([P, tiles, EXPERTS]), ALU.mult))
            step(nc.vector.reduce_max(lmax[:], chosen[:], AX_X))
            nc.vector.tensor_tensor(chosen[:], chosen[:], over_rows(lmax), ALU.is_equal).then_inc(chosen_ready, 1)
            dve.wait_ge(counted, 1)
            step(nc.vector.tensor_copy(count_et[:], tile_counts.rearrange("p (t e) -> p e t", t=tiles)))
            step(nc.vector.tensor_tensor_scan(upto[:].rearrange("p e t -> p (e t)"), ones[:, 0:EXPERTS * tiles],
                                              count_et[:].rearrange("p e t -> p (e t)"), 0.0, ALU.mult, ALU.add))
            step(nc.vector.tensor_copy(rows_of[:], upto[:, :, tiles - 1]))
            step(nc.vector.tensor_tensor(upto[:], upto[:], count_et[:], ALU.subtract))
            step(nc.vector.tensor_tensor(rows_of[:], rows_of[:], upto[:, :, 0], ALU.subtract))
            step(nc.vector.tensor_tensor(compare[:], starts[:, None, :].to_broadcast([P, EXPERTS, blocks]),
                                         rows_of[:, :, None].to_broadcast([P, EXPERTS, blocks]), ALU.is_lt))
            step(nc.vector.reduce_sum(padded[:], compare[:], AX_X))
            step(nc.vector.tensor_scalar(padded[:], padded[:], float(BLOCK), None, ALU.mult))
            step(nc.vector.tensor_tensor_scan(padded_end[:], ones[:, 0:EXPERTS], padded[:], 0.0, ALU.mult, ALU.add))
            step(nc.vector.tensor_tensor(shift[:], padded_end[:], padded[:], ALU.subtract))
            step(nc.vector.tensor_tensor(shift[:], shift[:], upto[:, :, 0], ALU.subtract))
            step(nc.vector.tensor_tensor(upto[:], upto[:], shift[:, :, None].to_broadcast([P, EXPERTS, tiles]),
                                         ALU.add))
            step(nc.vector.tensor_tensor(spots[:], upto[:].rearrange("p e t -> p t e"),
                                         tile_ranks.rearrange("p (t e) -> p t e", t=tiles), ALU.add))
            step(nc.vector.tensor_tensor(spots[:], spots[:], chosen[:], ALU.mult))
            step(nc.vector.reduce_sum(position[:], spots[:], AX_X))
            nc.vector.tensor_copy(position_i[:], position[:]).then_inc(positions_ready, 1)
            step(nc.vector.tensor_tensor(compare_b[:], padded_end[:, None, :].to_broadcast([P, blocks, EXPERTS]),
                                         starts[:, :, None].to_broadcast([P, blocks, EXPERTS]), ALU.is_le))
            step(nc.vector.reduce_sum(block_expert[:], compare_b[:], AX_X))
            nc.vector.tensor_scalar(block_expert_i[:], block_expert[:], float(EXPERTS - 1), None,
                                    ALU.min).then_inc(block_expert_ready, 1)

            def experts_mid(s, slot):
                dve.wait_ge(expert_in[slot], 16 * nth_of(s, slot))
                w = expert_w[slot]
                for c in range(FC):
                    if c % 2 == 0:
                        dve.wait_ge(mid_full, 2 * s + c // 2 + 1)
                    nc.vector.tensor_scalar(mid[slot][:, c, :], mid_bank(slot, c), w[:, EB1 + c:EB1 + c + 1], 0.0,
                                            ALU.add, ALU.max).then_inc(mid_ready, 1)
                dve.wait_ge(y_full, s + 1)
                nc.vector.tensor_scalar(y_T[slot][:], shared[1][:, 0:BLOCK], w[:, EB2:EB2 + 1], None,
                                        ALU.add).then_inc(yT_ready, 1)

            for_blocks(dve, experts_mid)
            for g in range(groups):
                dve.wait_ge(gathered[g], 16 * TILES)
                nc.vector.tensor_tensor(total[:, g * TILES:(g + 1) * TILES, :], total[:, g * TILES:(g + 1) * TILES, :],
                                        expert_rows[:, g * TILES:(g + 1) * TILES, :], ALU.add).then_inc(group_done, 1)

        @block.tensor
        def _(pe):
            def claim(s, name):
                b = s.bank(name)
                wait(pe, bank_free[b], s.full(name) - 1)
                return shared[b]

            def done(s, name, ins):
                ins.then_inc(bank_full[s.bank(name)], 1)

            def turn(bank, rows):
                for t in range(TILES):
                    last = nc.tensor.transpose(bank[:, t * P:(t + 1) * P], rows[:, t, :], ident[:])
                return last

            def mm(to, lhsT, rhs, start=True, stop=True):
                return nc.tensor.matmul(to, lhsT, rhs, start=start, stop=stop)

            def rows_twice(to, T, b, w):
                for half in range(2):
                    last = mm(to[half * SEQ:(half + 1) * SEQ], T[:, b * SEQ:(b + 1) * SEQ], w)
                return last

            def scores1(s, p):
                wait(pe, score1_free, s.item1(p))
                for h in range(HP):
                    for b in range(PER_TILE):
                        at = p * P + b * SEQ
                        last = mm(score1[b * SEQ:(b + 1) * SEQ, 2 * h:2 * h + 2, :], qT[:, h, at:at + SEQ],
                                  kblock[:, PER_TILE * p + b])
                last.then_inc(score1_full, 1)

            def scores2(s, p):
                wait(pe, score2_free, s.item2(p))
                pe.wait_ge(spread_ready, s.item2(p) + 1)
                for half in range(2):
                    for b in range(PER_TILE):
                        at = p * P + b * SEQ
                        hs = slice(half * HEADS // 2, (half + 1) * HEADS // 2)
                        last = mm(score2[b * SEQ:(b + 1) * SEQ, hs, :], q2T[:, at:at + SEQ],
                                  kspread[:, p % 2, b, hs, :])
                last.then_inc(score2_full, 1)

            def turn_probs(which, s, p):
                prob, ready, item = (prob1, prob1_ready, s.item1(p)) if which == "1" else \
                    (prob2, prob2_ready, s.item2(p))
                pe.wait_ge(ready, item + 1)
                wait(pe, tr_free, tr_index(s, which, p))
                for h in range(HP):
                    last = nc.tensor.transpose(transposed[:, h, :], prob[:, 2 * h:2 * h + 2, :], ident[:])
                last.then_inc(tr_full, 1)

            def values1(s, p):
                pe.wait_ge(tr_free, tr_index(s, "1", p) + 1)
                for b in range(PER_TILE):
                    name = f"o1{'ab'[b]}{p}"
                    bank = claim(s, name)
                    done(s, name, mm(bank[:], vblock[:, PER_TILE * p + b], pT1[:, :, b * SEQ:(b + 1) * SEQ]))

            def values2(s, p):
                pe.wait_ge(tr_free, tr_index(s, "2", p) + 1)
                bank = claim(s, f"o2{p}")[:, 0:PER_TILE * P].rearrange("p (h b c) -> p h b c", h=HP, b=PER_TILE)
                for h in range(HP):
                    last = mm(bank[:, h], pT2[:, h, :],
                              v2block[:, PER_TILE * p:PER_TILE * (p + 1), h].rearrange("p b c d -> p b (c d)"))
                done(s, f"o2{p}", last)

            pe.wait_ge(const_ready, 1)
            pe.wait_ge(rows_normed, 1)
            for b, rows in enumerate((xh, ch)):
                turn(shared[b], rows).then_inc(bank_full[b], 1)
            pe.wait_ge(weights_in, WEIGHTS_IN)
            pe.wait_ge(half_w, 1)

            def body(s):
                if s.attn1:
                    for b in range(2):
                        pe.wait_ge(bank_free[b], s.used[b])
                    done(s, "K", mm(claim(s, "K")[:], wk1_s[:].rearrange("p a d -> p (a d)"), cnT[:]))
                    bank = claim(s, "V")
                    for b in range(GB):
                        last = rows_twice(bank[:, b * D1:(b + 1) * D1], cnT, b, wv1_s[:])
                    done(s, "V", last)
                if s.attn2:
                    if not s.attn1:
                        for b in range(2):
                            pe.wait_ge(bank_free[b], s.used[b])
                    done(s, "Y", turn(claim(s, "Y"), yT[:].rearrange("p (t d) -> p t d", t=TILES)))
                for h in range(HP):
                    if h == HP // 2 and s.attn2:
                        pe.wait_ge(hn_ready, s.g)
                        done(s, "H", turn(claim(s, "H"), hn))
                    if s.attn1:
                        done(s, f"Q{h}", mm(claim(s, f"Q{h}")[:], wq1_s[:, h * P:(h + 1) * P], xnT[:]))
                if s.attn2:
                    wait_read(pe, s, "H")
                    done(s, "q2", mm(claim(s, "q2")[:], wq2_s[:], hnT[:]))
                    done(s, "k2", mm(claim(s, "k2")[:], wk2_s[:], hnT[:]))
                    for half, name in enumerate(("v2a", "v2b")):
                        bank = claim(s, name)
                        for b in range(GB // 2):
                            last = rows_twice(bank[:, b * P:(b + 1) * P], hnT, half * GB // 2 + b, wv2_s[:])
                        done(s, name, last)
                if s.attn1:
                    for name in (f"Q{HP - 2}", f"Q{HP - 1}"):
                        wait_read(pe, s, name)
                for p in range(TILES):
                    if s.attn1:
                        scores1(s, p)
                        if p:
                            values1(s, p - 1)
                    if s.attn2 and p:
                        turn_probs("2", s, p - 1)
                    if s.attn1:
                        for name, at in ((f"fh{p}", 0), (f"fg{p}", FF)):
                            done(s, name, mm(claim(s, name)[:], wff1_s[:, at + p * P:at + (p + 1) * P], xnT[:]))
                    if s.attn2 and p:
                        values2(s, p - 1)
                    if s.attn2:
                        if p == 0:
                            for name in ("v2a", "v2b"):
                                wait_read(pe, s, name)
                        scores2(s, p)
                    if s.attn1:
                        turn_probs("1", s, p)
                if s.attn1:
                    values1(s, TILES - 1)
                if s.attn2:
                    turn_probs("2", s, TILES - 1)
                if s.prepare:
                    pe.wait_ge(rows_normed, s.g + 2)
                    done(s, "X", turn(claim(s, "X"), xh))
                    done(s, "C", turn(claim(s, "C"), ch))
                if s.attn2:
                    values2(s, TILES - 1)
                    wait_read(pe, s, f"o2{TILES - 1}")
                    done(s, "O", turn(claim(s, "O"), o2))
                    wait_read(pe, s, "O")
                    bank = claim(s, "P")
                    for t in range(TILES):
                        last = mm(bank[:, t * P:(t + 1) * P], o2T[:, t * P:(t + 1) * P], wo2_s[:])
                    done(s, "P", last)
                if s.attn1:
                    bank = claim(s, "W")
                    for c in range(HP):
                        mm(bank[:], wo1_s[:, c, :], oT[:, c, :], start=(c == 0), stop=False)
                    for c in range(FC):
                        last = mm(bank[:], wff2_s[:, c, :], ffT[:, c, :], start=False, stop=(c == FC - 1))
                    done(s, "W", last)
                if s.attn2:
                    pe.wait_ge(h2_ready, s.g)
                    done(s, "G", turn(claim(s, "G"), h2))
                    wait_read(pe, s, "G")
                    bank = claim(s, "L")
                    for t in range(TILES):
                        last = mm(bank[:, t * EXPERTS:(t + 1) * EXPERTS], h2T[:, t * P:(t + 1) * P], gw_s[:])
                    done(s, "L", last)

            run_pipeline(pe, body)

            pe.wait_ge(chosen_ready, 1)
            flat = chosen[:].rearrange("p t e -> p (t e)")
            mm(tile_ranks, below[:], flat)
            mm(tile_counts, ones[:, 0:P], flat).then_inc(counted, 1)

            def turn_block(s, slot):
                pe.wait_ge(block_in[slot], 16 * nth_of(s, slot))
                wait(pe, block_T, s)
                for a in range(BA):
                    last = nc.tensor.transpose(shared[0][:, a * P:(a + 1) * P], block_rows[slot][:, a, :], ident[:])
                last.then_inc(block_turned, 1)

            def turn_y(s, slot):
                pe.wait_ge(yT_ready, s + 1)
                wait(pe, y_rows_ready, s)
                for a in range(BA):
                    last = nc.tensor.transpose(transposed[:, a, :], y_T[slot][:, a * P:(a + 1) * P], ident[:])
                last.then_inc(y_turned, 1)

            def one_block(s, slot):
                pe.wait_ge(expert_in[slot], 16 * nth_of(s, slot))
                pe.wait_ge(block_T, s + 1)
                wait(pe, mid_ready, FC * (s - 1))
                w = expert_w[slot]
                for c in range(FC):
                    last = mm(mid_bank(slot, c), w[:, EW1 + c * P:EW1 + (c + 1) * P], blockT[slot])
                    if c % 2:
                        last.then_inc(mid_full, 1)
                if not (isinstance(s, int) and s == blocks - 1):
                    turn_block(s + 1, 1 - slot)
                wait(pe, yT_ready, s)
                for c in range(FC):
                    pe.wait_ge(mid_ready, FC * s + c + 1)
                    last = mm(shared[1][:, 0:BLOCK], w[:, EW2 + c * P:EW2 + (c + 1) * P], mid[slot][:, c, :],
                              start=(c == 0), stop=(c == FC - 1))
                last.then_inc(y_full, 1)
                if not (isinstance(s, int) and s == 0):
                    turn_y(s - 1, 1 - slot)

            turn_block(0, 0)
            for_blocks(pe, one_block)
            turn_y(blocks - 1, (blocks - 1) % 2)


def kernel(**inputs):
    import numpy as np

    import concourse.bacc as bacc
    from concourse.bass_utils import run_bass_kernel_spmd

    a = {k: np.asarray(v) for k, v in inputs.items()}
    f = {k[len("L0_ffn_"):]: v for k, v in a.items() if k.startswith("L0_ffn_")}
    c = {k[len("L0_xattn_"):]: v for k, v in a.items() if k.startswith("L0_xattn_")}
    shape = a["x"].shape
    width = shape[-1]
    w2 = f["w2"].reshape(EXPERTS, FC, P, P).transpose(0, 2, 1, 3).reshape(EXPERTS, P, FC * P)
    b1 = f["b1"].reshape(EXPERTS, FC, P).transpose(0, 2, 1)
    experts = np.concatenate([f["w1"], w2, b1, f["b2"][:, :, None]], axis=2)
    laid = {
        "x": a["x"].reshape(-1, width), "ctx": a["ctx_1024"].reshape(-1, width),
        "wq1": c["Wq"], "wk1": c["Wkv"][:, :D1], "wv1": c["Wkv"][:, D1:], "wo1": c["Wo"],
        "wff1": c["Wff1"], "wff2": c["Wff2"], "wq2": f["wq"], "wk2": f["wk"], "wv2": f["wv"], "wo2": f["wo"],
        "vectors": np.stack([c["ln_g"], c["ln_b"], c["cln_g"], c["cln_b"], f["ln1_g"], f["ln1_b"], f["ln2_g"],
                             f["ln2_b"], f["bq"], f["bk"]], axis=1),
        "bv": f["bv"], "bo": f["bo"], "gate_w": f["gate_w"], "gate_b": f["gate_b"], "experts": experts,
    }
    nc = bacc.Bacc("TRN2", target_bir_lowering=False, num_devices=1)
    arrays, args = {}, []
    for name, v in laid.items():
        v = np.ascontiguousarray(v)
        arrays[f"in_{name}"] = v
        args.append(nc.dram_tensor(f"in_{name}", v.shape, mybir.dt.from_np(v.dtype), kind="ExternalInput").ap())
    args.append(nc.dram_tensor("out_x", arrays["in_x"].shape, F32, kind="ExternalOutput").ap())
    build(nc, *args)
    r = run_bass_kernel_spmd(nc, [arrays], core_ids=[0])
    return r.results[0]["out_x"].reshape(shape)
```

```python
from contextlib import ExitStack

import concourse.bass as bass
from concourse import mybir
from concourse.alu_op_type import AluOpType as ALU

F32 = mybir.dt.float32
I32 = mybir.dt.int32
ACT = mybir.ActivationFunctionType
AX_X = mybir.AxisListType.X

P = 128
SEQ = 64
PER_TILE = P // SEQ
TILES = 4
GT = TILES * P
GB = GT // SEQ
HEADS = 16
HP = HEADS // 2
D1 = 64
D2 = P // HEADS
FF = 512
FC = FF // P
EXPERTS = 8
BLOCK = 128
BA = BLOCK // P
WIDE = 128
PAIRS = 3
EPS = 1e-5
SCALE1 = float(D1) ** -0.5
SCALE2 = float(D2) ** -0.5
LN_G, LN_B, CLN_G, CLN_B, LN1_G, LN1_B, LN2_G, LN2_B, BQ, BK = range(10)
EW1, EW2, EB1, EB2, EN = 0, FF, FF + FC * P, FF + FC * P + FC, FF + FC * P + FC + P
RN, RT, RI, ROW = 0, P, 2 * P, 2 * P + 1
RANKS_AT = 4
SLOTS = 6


def psum_uses(attn1, attn2, prepare):
    uses = []
    if attn2:
        uses += ["Y"]
    if attn1:
        uses += ["K", "V"] + [f"Q{h}" for h in range(HP)]
    if attn2:
        uses += ["H"]
    for p in range(TILES):
        if attn2 and p == 0:
            uses += ["k2", "q2", "v2a", "v2b"]
        if attn1:
            uses += [f"fg{p}", f"fh{p}"]
        if attn1 and p:
            uses += [f"o1a{p - 1}", f"o1b{p - 1}"]
        if attn2 and p:
            uses += [f"o2{p - 1}"]
    if attn1:
        uses += [f"o1a{TILES - 1}", f"o1b{TILES - 1}"]
    if attn2:
        uses += [f"o2{TILES - 1}", "O", "P"]
    if prepare:
        uses += ["X"]
    if attn2:
        uses += ["G"]
    if prepare:
        uses += ["C"]
    return [(name, at % 2) for at, name in enumerate(uses)]


MIDDLE_VECTOR_STEPS = 43


class Step:

    def __init__(self, g, attn1, attn2, prepare, route, before):
        self.g, self.attn1, self.attn2, self.prepare, self.route = g, attn1, attn2, prepare, route
        self.uses = psum_uses(attn1, attn2, prepare)
        self.used = [before(0), before(1)]

    def bank(self, name):
        return dict(self.uses)[name]

    def full(self, name):
        bank = self.bank(name)
        return self.used[bank] + [n for n, b in self.uses if b == bank].index(name) + 1

    def item1(self, p):
        return TILES * self.g + p

    def item2(self, p):
        return TILES * (self.g - 1) + p


def wait(engine, semaphore, value):
    if isinstance(value, int) and value <= 0:
        return
    engine.wait_ge(semaphore, value)


def build(nc, x, ctx_in, wq1, wk1, wv1, wo1, wff1, wff2, wq2, wk2, wv2, wo2, vectors, bv, bo, gate_w,
          gate_b, experts, out):
    tokens = x.shape[0]
    groups = tokens // GT
    tiles = tokens // P
    blocks = tokens // BLOCK + EXPERTS - 1
    room = tokens + BLOCK
    idle_at = EXPERTS * room

    sorted_in = nc.dram_tensor("sorted_in", [idle_at + BLOCK, ROW], F32, kind="Internal").ap()

    es = ExitStack()
    with es:
        def sb(name, shape, dt=F32):
            return es.enter_context(nc.sbuf_tensor(name, shape, dt))

        def ps(name, shape):
            return es.enter_context(nc.psum_tensor(name, shape, F32))

        def sem(name):
            return es.enter_context(nc.semaphore(name))

        wq1_s = sb("wq1_s", [P, HEADS * D1])
        wk1_s = sb("wk1_s", [P, 2, D1])
        wv1_s = sb("wv1_s", [P, D1])
        wo1_s = sb("wo1_s", [P, HP, P])
        wff1_s = sb("wff1_s", [P, 2 * FF])
        wff2_s = sb("wff2_s", [P, FC, P])
        wq2_s = sb("wq2_s", [P, P])
        wk2_s = sb("wk2_s", [P, P])
        wv2_s = sb("wv2_s", [P, P])
        wo2_s = sb("wo2_s", [P, P])
        vec = sb("vec", [P, 10])
        bv_s = sb("bv_s", [P, P])
        bo_s = sb("bo_s", [P, P])
        gw_s = sb("gw_s", [P, WIDE])
        gb_s = sb("gb_s", [P, EXPERTS])
        ident = sb("ident", [P, P])
        head_mask = sb("head_mask", [P, HEADS])
        below = sb("below", [P, P])
        ones = sb("ones", [P, 256])
        first_wins = sb("first_wins", [P, EXPERTS])
        starts = sb("starts", [P, blocks])
        room_at = sb("room_at", [P, EXPERTS])
        filling = sb("filling", [P, BA, ROW])
        ints = sb("ints", [P, EXPERTS + blocks], I32)
        ints_at = sb("ints_at", [P, EXPERTS], I32)
        ints_id = sb("ints_id", [P, TILES + BA], I32)

        x_s = sb("x_s", [P, tiles, P])
        expert_all = sb("expert_all", [P, EXPERTS, EN])
        c_s = expert_all[:].rearrange("p e n -> p (e n)")[:, 0:tiles * P].rearrange("p (t d) -> p t d", t=tiles)
        apart = -(-tiles * P // EN)

        xh = sb("xh", [P, TILES, P])
        ch = sb("ch", [P, TILES, P])
        xnT = sb("xnT", [P, GT])
        cnT = sb("cnT", [P, GT])
        kblock = sb("kblock", [P, GB, 2, SEQ])
        vblock = sb("vblock", [P, GB, 2, D1])
        qT = sb("qT", [P, HP, GT])
        oT = sb("oT", [P, HP, GT])
        tanh_g = sb("tanh_g", [P, GT])
        ffT = sb("ffT", [P, FC, GT])
        prob1 = sb("prob1", [P, HEADS, SEQ])
        prob2 = sb("prob2", [P, HEADS, SEQ])
        pT1 = sb("pT1", [P, HP, P])
        pT2 = sb("pT2", [P, HP, P])
        yT = sb("yT", [P, GT])
        x1 = sb("x1", [P, TILES, P])
        z = sb("z", [P, TILES, P])
        hn = sb("hn", [P, TILES, P])
        hnT = sb("hnT", [P, GT])
        q2T = sb("q2T", [P, GT])
        k2T = sb("k2T", [P, GT])
        v2block = sb("v2block", [P, GB, HP + PAIRS - 1, 2, D2 + 1])
        kspread = sb("kspread", [P, 2, PER_TILE, HEADS, SEQ])
        o2 = sb("o2", [P, TILES, P])
        o2T = q2T
        h2T = hnT
        max1 = sb("max1", [P, HEADS])
        max2 = sb("max2", [P, HEADS])
        sum1 = sb("sum1", [P, HEADS])
        inv1 = sb("inv1", [P, HEADS])
        inv2 = sb("inv2", [P, 2, HEADS])
        rows_out = sb("rows_out", [P, TILES, ROW])
        logits = sb("logits", [P, TILES, EXPERTS])
        chosen_wide = sb("chosen_wide", [P, WIDE])
        chosen = chosen_wide[:, 0:TILES * EXPERTS].rearrange("p (t e) -> p t e", t=TILES)
        lmax = sb("lmax", [P, TILES])
        rank_count = sb("rank_count", [P, 2, TILES, EXPERTS])
        next_at = sb("next_at", [P, TILES + 1, EXPERTS])
        spots = sb("spots", [P, TILES, EXPERTS])
        position = sb("position", [P, TILES])
        position_i = sb("position_i", [P, TILES], I32)
        filling_at = sb("filling_at", [P, EXPERTS], I32)
        rows_of = sb("rows_of", [P, EXPERTS])
        padded = sb("padded", [P, EXPERTS])
        padded_end = sb("padded_end", [P, EXPERTS])
        compare = sb("compare", [P, EXPERTS, blocks])
        compare_b = sb("compare_b", [P, blocks, EXPERTS])
        jumps = sb("jumps", [P, blocks, EXPERTS])
        block_expert = sb("block_expert", [P, blocks])
        block_expert_i = sb("block_expert_i", [P, blocks], I32)
        block_at = sb("block_at", [P, blocks])
        block_at_i = sb("block_at_i", [P, blocks], I32)
        token_i = sb("token_i", [P, SLOTS, BA], I32)
        stat, mv, var, rstd, shift_n = ({which: sb(f"{name}_{which}", [P, n] + rest)
                                         for which, n in (("rows", TILES), ("next", 2 * TILES))}
                                        for name, rest in (("stat", [6]), ("mv", [2]), ("var", []), ("rstd", []),
                                                           ("shift", [])))
        minus_half = sb("minus_half", [P, 2 * TILES])
        carrier = sb("carrier", [P, 1])

        def from_buffer(buffer, at, shape):
            names = "abcd"[:len(buffer.shape) - 1]
            flat = buffer[:].rearrange(f"p {' '.join(names)} -> p ({' '.join(names)})")
            if len(shape) == 1:
                return flat[:, at:at + shape[0]]
            return flat[:, at:at + shape[0] * shape[1]].rearrange("p (a b) -> p a b", a=shape[0])

        expert_w = [from_buffer(buffer, i * EN, [EN]) for buffer in (oT, kspread) for i in range(SLOTS // 2)]
        block_rows = [from_buffer(qT, i * BA * ROW, [BA, ROW]) for i in range(SLOTS)]
        y_rows = [from_buffer(qT, SLOTS * BA * ROW + i * BLOCK, [BA, P]) for i in range(SLOTS)]
        blockT = [from_buffer(kspread, SLOTS // 2 * EN + i * BLOCK, [BLOCK]) for i in range(2)]
        mid = [from_buffer(ffT, i * FC * BLOCK, [FC, BLOCK]) for i in range(2)]

        score1 = ps("score1", [P, HEADS, SEQ])
        score2 = ps("score2", [P, HEADS, SEQ])
        transposed = ps("transposed", [P, HP, P])
        shared = [ps(f"shared{i}", [P, GT]) for i in range(2)]
        side_y, side_router = (score1[:].rearrange("p h j -> p (h j)")[:, b * GT:(b + 1) * GT] for b in range(2))

        weights_in = sem("weights_in")
        rows0_in = sem("rows0_in")
        rows_in = sem("rows_in")
        filled = sem("filled")
        const_step = sem("const_step")
        const_ready = sem("const_ready")
        half_w = sem("half_w")
        var_ready = sem("var_ready")
        rstd_ready = sem("rstd_ready")
        next_var_ready = sem("next_var_ready")
        next_rstd_ready = sem("next_rstd_ready")
        next_shift_ready = sem("next_shift_ready")
        x_once = sem("x_once")
        next_rows = sem("next_rows")
        dve_done = sem("dve_done")
        bank_full = [sem(f"bank_full{i}") for i in range(2)]
        bank_free = [sem(f"bank_free{i}") for i in range(2)]
        score1_full = sem("score1_full")
        score1_free = sem("score1_free")
        exp1_done = sem("exp1_done")
        inv1_ready = sem("inv1_ready")
        prob1_ready = sem("prob1_ready")
        score2_full = sem("score2_full")
        score2_free = sem("score2_free")
        exp2_done = sem("exp2_done")
        tr_full = sem("tr_full")
        tr_free = sem("tr_free")
        tanh_done = sem("tanh_done")
        hn_ready = sem("hn_ready")
        spread_ready = sem("spread_ready")
        h2_ready = sem("h2_ready")
        y1_full = sem("y1_full")
        y1_read = sem("y1_read")
        logits_full = sem("logits_full")
        chosen_ready = sem("chosen_ready")
        ranks_full = sem("ranks_full")
        ranks_read = sem("ranks_read")
        positions_ready = sem("positions_ready")
        filling_at_ready = sem("filling_at_ready")
        blocks_ready = sem("blocks_ready")
        scattered = sem("scattered")
        experts_in = sem("experts_in")
        block_in = [sem(f"block_in{i}") for i in range(SLOTS)]
        block_turned = sem("block_turned")
        block_T = sem("block_T")
        expert_w_ready = sem("expert_w_ready")
        mid_full = sem("mid_full")
        mid_ready = sem("mid_ready")
        y_full = sem("y_full")
        rest_ready = sem("rest_ready")
        y_ready = sem("y_ready")
        out_stored = [sem(f"out_stored{i}") for i in range(SLOTS)]

        FIRST = dict(attn1=True, attn2=False, prepare=True, route=False)
        SECOND = dict(attn1=True, attn2=True, prepare=True, route=False)
        MID = dict(attn1=True, attn2=True, prepare=True, route=True)
        LAST = dict(attn1=True, attn2=True, prepare=False, route=True)
        DRAIN = dict(attn1=False, attn2=True, prepare=False, route=True)
        ROUTE = dict(attn1=False, attn2=False, prepare=False, route=True)

        def in_bank(kind, b):
            return sum(bank == b for _, bank in psum_uses(kind["attn1"], kind["attn2"], kind["prepare"]))

        def first_step():
            return Step(0, before=lambda b: 1, **FIRST)

        def second_step():
            return Step(1, before=lambda b: 1 + in_bank(FIRST, b), **SECOND)

        def at_middle(g, b):
            return 1 + in_bank(FIRST, b) + in_bank(SECOND, b) + (g - 2) * in_bank(MID, b)

        def middle_step(g):
            return Step(g, before=lambda b: at_middle(g, b), **MID)

        def last_step():
            return Step(groups - 1, before=lambda b: at_middle(groups - 1, b), **LAST)

        def drain_step():
            return Step(groups, before=lambda b: at_middle(groups - 1, b) + in_bank(LAST, b), **DRAIN)

        def route_step():
            return Step(groups + 1, before=lambda b: at_middle(groups - 1, b) + in_bank(LAST, b)
                        + in_bank(DRAIN, b), **ROUTE)

        def wait_read(engine, s, name):
            engine.wait_ge(bank_free[s.bank(name)], s.full(name))

        def group_rows(rows, g):
            return rows[:, bass.ds(g * TILES, TILES), :] if not isinstance(g, int) else \
                rows[:, g * TILES:(g + 1) * TILES, :]

        def run_pipeline(engine, body):
            body(first_step())
            body(second_step())
            with engine.Fori(2, groups - 1) as g:
                body(middle_step(g))
            body(last_step())
            body(drain_step())
            body(route_step())

        def transposes_before(s):
            if isinstance(s.g, int) and s.g == 0:
                return 0
            return TILES + (s.g - 1) * 2 * TILES

        tr_order = {}
        for kind, (a1, a2) in (("first", (True, False)), ("mid", (True, True)), ("drain", (False, True))):
            order = []
            for p in range(TILES):
                if a2 and p:
                    order.append(("2", p - 1))
                if a1:
                    order.append(("1", p))
            if a2:
                order.append(("2", TILES - 1))
            tr_order[(a1, a2)] = order

        def tr_index(s, which, p):
            return transposes_before(s) + tr_order[(s.attn1, s.attn2)].index((which, p))

        def mid_bank(slot, c):
            at = c // 2 * GT + c % 2 * BLOCK
            return (score1, score2)[slot][:].rearrange("p h j -> p (h j)")[:, at:at + BLOCK]

        def turned_bank(slot):
            return transposed[:].rearrange("p h c -> p (h c)")[:, slot % 2 * GT:slot % 2 * GT + BLOCK]

        def y_bank(slot):
            return shared[slot % 2][:, 0:BLOCK]

        block = es.enter_context(nc.Block())

        WEIGHTS_IN = 16 * 16

        def for_blocks(engine, run):
            for s in range(SLOTS):
                run(s, s, 1)
            with engine.Fori(1, blocks // SLOTS) as i:
                for slot in range(SLOTS):
                    run(SLOTS * i + slot, slot, i + 1)
            for s in range(blocks // SLOTS * SLOTS, blocks):
                run(s, s % SLOTS, s // SLOTS + 1)

        def put_filling(engine, some):
            engine.wait_ge(filling_at_ready, 1)
            for e in some:
                at = engine.value_load(filling_at[0:1, e:e + 1], min_val=0, max_val=idle_at - BLOCK)
                engine.dma_start(sorted_in[bass.ds(at, BLOCK), :].rearrange("(p a) d -> p a d", p=P),
                                 filling[:]).then_inc(filled, 16)

        @block.sync
        def _(sp):
            xv = x.rearrange("(t p) d -> p t d", p=P)
            cv = ctx_in.rearrange("(t p) d -> p t d", p=P)
            sp.dma_start(x_s[:, 0:TILES, :], xv[:, 0:TILES, :]).then_inc(rows0_in, 16)
            sp.dma_start(c_s[:, 0:TILES, :], cv[:, 0:TILES, :]).then_inc(rows0_in, 16)
            sp.dma_start(vec[:], vectors).then_inc(weights_in, 16)
            for half in range(2):
                sp.dma_start(wk1_s[:, half, :], wk1).then_inc(weights_in, 16)
            sp.dma_start(wv1_s[:], wv1).then_inc(weights_in, 16)
            sp.dma_start(wq1_s[:], wq1).then_inc(weights_in, 16)
            sp.dma_start(wff1_s[:], wff1).then_inc(weights_in, 16)
            sp.dma_start(wff2_s[:], wff2.rearrange("(c p) n -> p c n", p=P)).then_inc(weights_in, 16)
            sp.dma_start(wo1_s[:], wo1.rearrange("(c p) n -> p c n", p=P)).then_inc(weights_in, 16)
            for to, of in ((wq2_s, wq2), (wk2_s, wk2), (wv2_s, wv2), (wo2_s, wo2)):
                sp.dma_start(to[:], of).then_inc(weights_in, 16)
            sp.wait_ge(const_ready, 1)
            sp.dma_start(gw_s[:, 0:EXPERTS], gate_w).then_inc(weights_in, 16)
            for to, of in ((bv_s, bv), (bo_s, bo), (gb_s, gate_b)):
                sp.dma_start(to[:], of.partition_broadcast(P)).then_inc(weights_in, 16)
            sp.dma_start(x_s[:, TILES:, :], xv[:, TILES:, :]).then_inc(rows_in, 16)
            sp.dma_start(c_s[:, TILES:, :], cv[:, TILES:, :]).then_inc(rows_in, 16)
            sp.dma_start(sorted_in[idle_at:idle_at + BLOCK, :].rearrange("(p a) d -> p a d", p=P), filling[:]).then_inc(
                filled, 16)
            sp.dma_start(expert_all[:, apart:, :], experts[apart:].rearrange("e p n -> p e n")).then_inc(experts_in, 16)
            sp.wait_ge(next_rows, 2 * groups)
            sp.dma_start(expert_all[:, 0:apart, :], experts[0:apart].rearrange("e p n -> p e n")).then_inc(
                experts_in, 16)

            def load_block(s, slot, nth):
                wait(sp, y_ready, s - SLOTS + 1)
                at = sp.value_load(block_at_i[0:1, bass.ds(s, 1)], min_val=0, max_val=idle_at)
                sp.dma_start(block_rows[slot], sorted_in[bass.ds(at, BLOCK), :].rearrange(
                    "(p a) d -> p a d", p=P)).then_inc(block_in[slot], 16)

            put_filling(sp, range(0, EXPERTS, 2))
            sp.wait_ge(blocks_ready, 1)
            sp.wait_ge(scattered, 16 * tiles)
            sp.wait_ge(filled, 16 * (1 + EXPERTS))
            for_blocks(sp, load_block)
            for slot in range(SLOTS):
                sp.wait_ge(out_stored[slot], 16 * BA * len(range(slot, blocks, SLOTS)))

        @block.gpsimd
        def _(pool):
            steps = [0]

            def step(ins):
                steps[0] += 1
                ins.then_inc(const_step, 1)
                pool.wait_ge(const_step, steps[0])

            nc.gpsimd.memset(ident[:], 0.0)
            nc.gpsimd.memset(head_mask[:], 1.0)
            nc.gpsimd.memset(kblock[:], 0.0)
            nc.gpsimd.memset(vblock[:], 0.0)
            nc.gpsimd.memset(v2block[:], 0.0)
            nc.gpsimd.memset(ones[:], 1.0)
            nc.gpsimd.memset(minus_half[:], -0.5)
            nc.gpsimd.memset(filling[:], 0.0)
            nc.gpsimd.memset(chosen_wide[:], 0.0)
            nc.gpsimd.memset(gw_s[:], 0.0)
            step(nc.gpsimd.memset(below[:], 1.0))
            for c in range(2):
                step(nc.gpsimd.memset(v2block[c * SEQ:(c + 1) * SEQ, :, 0:HP, c, D2:D2 + 1], 1.0))
            step(nc.gpsimd.affine_select(out=ident[:], in_=ident[:], compare_op=ALU.not_equal, fill=1.0,
                                         base=0, pattern=[[-1, P]], channel_multiplier=1))
            step(nc.gpsimd.affine_select(out=head_mask[:], in_=head_mask[:], compare_op=ALU.is_ge, fill=0.0,
                                         base=0, pattern=[[-D2, HEADS]], channel_multiplier=1))
            step(nc.gpsimd.affine_select(out=head_mask[:], in_=head_mask[:], compare_op=ALU.is_ge, fill=0.0,
                                         base=D2 - 1, pattern=[[D2, HEADS]], channel_multiplier=-1))
            step(nc.gpsimd.affine_select(out=below[:], in_=below[:], compare_op=ALU.is_gt, fill=0.0,
                                         base=0, pattern=[[1, P]], channel_multiplier=-1))
            nc.gpsimd.iota(ints[:, 0:EXPERTS], pattern=[[-1, EXPERTS]], base=EXPERTS, channel_multiplier=0)
            nc.gpsimd.iota(ints[:, EXPERTS:], pattern=[[BLOCK, blocks]], base=0, channel_multiplier=0)
            nc.gpsimd.iota(ints_at[:], pattern=[[room, EXPERTS]], base=0, channel_multiplier=0)
            nc.gpsimd.iota(ints_id[:, 0:TILES], pattern=[[P, TILES]], base=-GT, channel_multiplier=1)
            step(nc.gpsimd.iota(ints_id[:, TILES:], pattern=[[1, BA]], base=tokens, channel_multiplier=BA))
            nc.gpsimd.tensor_copy(first_wins[:], ints[:, 0:EXPERTS])
            nc.gpsimd.tensor_copy(starts[:], ints[:, EXPERTS:])
            nc.gpsimd.tensor_copy(room_at[:], ints_at[:])
            nc.gpsimd.tensor_copy(next_at[:, 0, :], ints_at[:])
            nc.gpsimd.tensor_copy(rows_out[:, :, RI], ints_id[:, 0:TILES])
            nc.gpsimd.tensor_copy(filling[:, :, RI], ints_id[:, TILES:]).then_inc(const_ready, 1)

            def spread(s, p):
                for b in range(PER_TILE):
                    at = (PER_TILE * p + b) * SEQ
                    ins = nc.gpsimd.tensor_tensor(
                        kspread[:, p % 2, b], k2T[:, None, at:at + SEQ].to_broadcast([P, HEADS, SEQ]),
                        head_mask[:, :, None].to_broadcast([P, HEADS, SEQ]), ALU.mult)
                ins.then_inc(spread_ready, 1)

            def normalise(prob, inv, inv_ready, count, ready):
                pool.wait_ge(inv_ready, count + 1)
                nc.gpsimd.tensor_tensor(prob[:], prob[:], inv[:, :, None].to_broadcast([P, HEADS, SEQ]),
                                        ALU.mult).then_inc(ready, 1)

            def inverse_root(which, n, ready, count, done):
                pool.wait_ge(ready, count)
                nc.gpsimd.tensor_tensor(rstd[which][:, 0:n], var[which][:, 0:n], minus_half[:, 0:n],
                                        ALU.pow).then_inc(done, 1)

            for turn, n in ((1, 2 * TILES), (2, TILES)):
                inverse_root("next", n, next_var_ready, turn, next_rstd_ready)

            def scatter(s):
                for t in range(TILES):
                    nc.gpsimd.indirect_dma_start(
                        out=sorted_in, out_offset=bass.IndirectOffsetOnAxis(ap=position_i[:, t:t + 1], axis=0),
                        in_=rows_out[:, t, :], in_offset=None).then_inc(scattered, 16)

            def body(s):
                if not (s.attn1 or s.attn2):
                    pool.wait_ge(positions_ready, groups)
                    scatter(s)
                    return
                if s.attn2:
                    for turn in (1, 2):
                        inverse_root("rows", TILES, var_ready, 3 * (s.g - 1) + turn, rstd_ready)
                    wait_read(pool, s, "k2")
                    spread(s, 0)
                for p in range(TILES):
                    if s.prepare and p == 0:
                        inverse_root("next", 2 * TILES, next_var_ready, 2 * (s.g + 1) + 1, next_rstd_ready)
                    if s.attn1:
                        normalise(prob1, inv1, inv1_ready, s.item1(p), prob1_ready)
                    if s.attn2 and p + 1 < TILES:
                        if p:
                            pool.wait_ge(score2_full, s.item2(p - 1) + 1)
                        spread(s, p + 1)
                if s.prepare:
                    if s.route:
                        pool.wait_ge(positions_ready, s.g - 1)
                    inverse_root("next", TILES, next_var_ready, 2 * (s.g + 1) + 2, next_rstd_ready)
                elif s.route:
                    pool.wait_ge(positions_ready, s.g - 1)
                if s.route:
                    scatter(s)
                if s.attn2:
                    inverse_root("rows", TILES, var_ready, 3 * s.g, rstd_ready)

            run_pipeline(pool, body)

            def block_out(s, slot, nth):
                pool.wait_ge(block_in[slot], 16 * nth)
                pool.wait_ge(expert_w_ready, s + 1)
                wait(pool, y_ready, s)
                rest = block_rows[slot][:, :, RT:RT + P]
                nc.gpsimd.tensor_tensor(rest, rest, expert_w[slot][:, None, EB2:EB2 + P].to_broadcast([P, BA, P]),
                                        ALU.add).then_inc(rest_ready, 1)
                if not (isinstance(s, int) and s == 0):
                    store(s - 1, (slot - 1) % SLOTS)

            def store(s, slot):
                for a in range(BA):
                    nc.gpsimd.indirect_dma_start(
                        out=out, out_offset=bass.IndirectOffsetOnAxis(ap=token_i[:, slot, a:a + 1], axis=0),
                        in_=y_rows[slot][:, a, :], in_offset=None, bounds_check=tokens - 1,
                        oob_is_err=False).then_inc(out_stored[slot], 16)

            for_blocks(pool, block_out)
            pool.wait_ge(y_ready, blocks)
            store(blocks - 1, (blocks - 1) % SLOTS)

        @block.scalar
        def _(act):
            def take(s, name):
                act.wait_ge(bank_full[s.bank(name)], s.full(name))
                return shared[s.bank(name)]

            def affine(to, bank, gain, bias):
                return nc.scalar.activation(to[:], bank[:], ACT.Identity, bias=vec[:, bias:bias + 1],
                                            scale=vec[:, gain:gain + 1])

            def free(s, name, ins):
                ins.then_inc(bank_free[s.bank(name)], 1)

            def copy_out(which, to, s, p):
                act.wait_ge(tr_full, tr_index(s, which, p) + 1)
                nc.scalar.copy(to[:, 0:HP // 2, :], transposed[:, 0:HP // 2, :])
                nc.scalar.copy(to[:, HP // 2:, :], transposed[:, HP // 2:, :]).then_inc(tr_free, 1)

            def out1(s, p):
                for b in range(PER_TILE):
                    bank = take(s, f"o1{'ab'[b]}{p}")
                    at = p * P + b * SEQ
                    free(s, f"o1{'ab'[b]}{p}",
                         nc.scalar.copy(oT[:, :, at:at + SEQ], bank[:].rearrange("p (h i) -> p h i", h=HP)))

            def normed(src, dst, at):
                for t in range(TILES):
                    last = nc.scalar.activation(dst[:, t, :], src[:, t, :], ACT.Identity,
                                                bias=shift_n["next"][:, at + t:at + t + 1],
                                                scale=rstd["next"][:, at + t:at + t + 1])
                return last

            def next_once(g):
                act.wait_ge(next_shift_ready, 2 * g + 1)
                normed(group_rows(x_s, g), xh, 0).then_inc(x_once, 1)

            def next_context(g):
                normed(group_rows(c_s, g), ch, TILES).then_inc(next_rows, 1)

            def next_twice(g):
                act.wait_ge(next_shift_ready, 2 * g + 2)
                normed(xh, xh, 0).then_inc(next_rows, 1)

            next_once(0)
            next_context(0)
            next_twice(0)
            act.wait_ge(weights_in, WEIGHTS_IN)
            act.wait_ge(const_ready, 1)
            for b, (to, gain, bias) in enumerate(((xnT, LN_G, LN_B), (cnT, CLN_G, CLN_B))):
                act.wait_ge(bank_full[b], 1)
                affine(to, shared[b], gain, bias).then_inc(bank_free[b], 1)
            act.wait_ge(rows_in, 32)

            def tanh(s, p):
                if p:
                    wait_read(act, s, f"fh{p - 1}")
                bank = take(s, f"fg{p}")
                nc.scalar.activation(tanh_g[:], bank[:], ACT.Tanh, scale=0.5).then_inc(tanh_done, 1)

            def route_in(s):
                act.wait_ge(ranks_full, s.g - 1)
                nc.scalar.copy(rank_count[:].rearrange("p w t e -> p w (t e)"), side_router[:, 0:2 * WIDE].rearrange(
                    "p (w n) -> p w n", w=2)[:, :, 0:TILES * EXPERTS]).then_inc(ranks_read, 1)

            def body(s):
                if s.attn1:
                    bank = take(s, "K")[:].rearrange("p (b j) -> p b j", b=GB)
                    nc.scalar.copy(kblock[0:SEQ, :, 0, :], bank[0:SEQ])
                    free(s, "K", nc.scalar.copy(kblock[SEQ:P, :, 1, :], bank[SEQ:P]))
                    bank = take(s, "V")[:].rearrange("p (b j) -> p b j", b=GB)
                    nc.scalar.copy(vblock[0:SEQ, :, 0, :], bank[0:SEQ])
                    free(s, "V", nc.scalar.copy(vblock[SEQ:P, :, 1, :], bank[SEQ:P]))
                if not (s.attn1 or s.attn2):
                    route_in(s)
                    return
                if s.route and not s.attn1:
                    route_in(s)
                if s.attn1:
                    for h in range(HP):
                        if s.route and h == RANKS_AT:
                            route_in(s)
                        free(s, f"Q{h}", nc.scalar.copy(qT[:, h, :], take(s, f"Q{h}")[:]))
                if s.attn2:
                    free(s, "H", affine(hnT, take(s, "H"), LN1_G, LN1_B))
                for p in range(TILES):
                    if s.attn1 and p:
                        tanh(s, p)
                    if s.attn2 and p == 0:
                        for name, to, bias in (("k2", k2T, BK), ("q2", q2T, BQ)):
                            free(s, name, nc.scalar.activation(to[:], take(s, name)[:], ACT.Identity,
                                                               bias=vec[:, bias:bias + 1]))
                    if s.attn1:
                        act.wait_ge(score1_free, s.item1(p) + 1)
                        nc.scalar.activation(prob1[:], prob1[:], ACT.Exp, scale=SCALE1).then_inc(exp1_done, 1)
                    if s.attn1 and p == 0:
                        tanh(s, p)
                        copy_out("1", pT1, s, p)
                    if s.attn2 and p:
                        copy_out("2", pT2, s, p - 1)
                    if s.attn1 and p:
                        out1(s, p - 1)
                    if s.attn2:
                        act.wait_ge(score2_free, s.item2(p) + 1)
                        nc.scalar.activation(prob2[:], prob2[:], ACT.Exp, scale=SCALE2).then_inc(exp2_done, 1)
                    if s.attn1 and p:
                        copy_out("1", pT1, s, p)
                    if s.prepare and p == 1:
                        next_once(s.g + 1)
                    if s.prepare and p == 2:
                        next_context(s.g + 1)
                if s.attn2:
                    copy_out("2", pT2, s, TILES - 1)
                if s.attn1:
                    out1(s, TILES - 1)
                if s.prepare:
                    next_twice(s.g + 1)
                if s.attn2:
                    free(s, "O", nc.scalar.copy(o2T[:], take(s, "O")[:]))
                if s.attn1:
                    act.wait_ge(y1_full, s.g + 1)
                    nc.scalar.copy(yT[:], side_y).then_inc(y1_read, 1)
                if s.prepare:
                    free(s, "X", affine(xnT, take(s, "X"), LN_G, LN_B))
                if s.attn2:
                    free(s, "G", affine(h2T, take(s, "G"), LN2_G, LN2_B))
                if s.prepare:
                    free(s, "C", affine(cnT, take(s, "C"), CLN_G, CLN_B))

            run_pipeline(act, body)

            put_filling(act, range(1, EXPERTS, 2))

            def expert_weights(s, slot):
                wait(act, y_ready, s - SLOTS + 1)
                e = act.value_load(block_expert_i[0:1, bass.ds(s, 1)], min_val=0, max_val=EXPERTS - 1)
                nc.scalar.copy(expert_w[slot], expert_all[:, bass.ds(e, 1), :].rearrange("p e n -> p (e n)")).then_inc(
                    expert_w_ready, 1)

            def turned_in(s, slot):
                act.wait_ge(block_turned, s + 1)
                nc.scalar.activation(blockT[slot % 2], turned_bank(slot), ACT.Identity,
                                     bias=vec[:, LN2_B:LN2_B + 1], scale=vec[:, LN2_G:LN2_G + 1]).then_inc(block_T, 1)

            def block_ahead(s, slot, nth):
                if not (isinstance(s, int) and s >= blocks - 1):
                    turned_in(s + 1, (slot + 1) % SLOTS)
                if not (isinstance(s, int) and s >= blocks - 2):
                    expert_weights(s + 2, (slot + 2) % SLOTS)

            act.wait_ge(blocks_ready, 1)
            act.wait_ge(experts_in, 32)
            expert_weights(0, 0)
            expert_weights(1, 1)
            turned_in(0, 0)
            for_blocks(act, block_ahead)

        @block.vector
        def _(dve):
            count = {"base": 0, "n": 0}

            def step(ins):
                count["n"] += 1
                ins.then_inc(dve_done, 1)
                dve.wait_ge(dve_done, count["base"] + count["n"])

            def statistics(which, tiles_of_rows, ready, count):
                for t, rows in enumerate(tiles_of_rows):
                    last = nc.vector.bn_stats(stat[which][:, t, :], rows)
                step(last)
                nc.vector.memset(carrier[:], 0.0)
                for t in range(len(tiles_of_rows)):
                    last = nc.vector.bn_aggr(mv[which][:, t, :], stat[which][:, t, :])
                step(last)
                n = len(tiles_of_rows)
                nc.vector.tensor_scalar(var[which][:, 0:n], mv[which][:, 0:n, 1], EPS, None, ALU.add).then_inc(ready, 1)
                dve.wait_ge(ready, count)

            def tiles_in(rows):
                return [rows[:, t, :] for t in range(TILES)]

            def norm(src, dst, count):
                statistics("rows", tiles_in(src), var_ready, count)
                return normed(src, dst, count)

            def normed(src, dst, count):
                dve.wait_ge(rstd_ready, count)
                for t in range(TILES):
                    last = nc.vector.tensor_scalar(dst[:, t, :], src[:, t, :], mv["rows"][:, t, 0:1],
                                                   rstd["rows"][:, t:t + 1], ALU.subtract, ALU.mult)
                return last

            def next_shift(n, count):
                dve.wait_ge(next_rstd_ready, count)
                nc.vector.scalar_tensor_tensor(out=shift_n["next"][:, 0:n], in0=mv["next"][:, 0:n, 0], scalar=-1.0,
                                               in1=rstd["next"][:, 0:n], op0=ALU.mult,
                                               op1=ALU.mult).then_inc(next_shift_ready, 1)
                dve.wait_ge(next_shift_ready, count)

            def next_first(g):
                wait(dve, next_rows, 2 * g)
                statistics("next", tiles_in(group_rows(x_s, g)) + tiles_in(group_rows(c_s, g)), next_var_ready,
                           2 * g + 1)

            def next_second(g):
                dve.wait_ge(x_once, g + 1)
                dve.wait_ge(next_rows, 2 * g + 1)
                statistics("next", tiles_in(xh), next_var_ready, 2 * g + 2)

            def less_max(score, mx, prob, free_sem):
                step(nc.vector.reduce_max(mx[:], score[:], AX_X))
                nc.vector.tensor_tensor(prob[:], score[:], mx[:, :, None].to_broadcast([P, HEADS, SEQ]),
                                        ALU.subtract).then_inc(free_sem, 1)

            def invert_sum(prob, sm, inv, ready):
                step(nc.vector.reduce_sum(sm[:], prob[:], AX_X))
                nc.vector.reciprocal(inv[:], sm[:]).then_inc(ready, 1)

            dve.wait_ge(rows0_in, 32)
            next_first(0)
            next_shift(2 * TILES, 1)
            next_second(0)
            next_shift(TILES, 2)
            dve.wait_ge(weights_in, WEIGHTS_IN)
            nc.vector.tensor_scalar(wff2_s[:], wff2_s[:], 0.5, None, ALU.mult).then_inc(half_w, 1)
            dve.wait_ge(rows_in, 32)
            dve.wait_ge(const_ready, 1)

            def values2_in(s):
                for half, name in enumerate(("v2a", "v2b")):
                    dve.wait_ge(bank_full[s.bank(name)], s.full(name))
                    bank = shared[s.bank(name)][:].rearrange("p (b h c d) -> p b h c d", b=GB // 2, h=HP, c=2)
                    bias = bv_s[:].rearrange("p (h c d) -> p h c d", h=HP, c=2)
                    to = v2block[:, half * GB // 2:(half + 1) * GB // 2, 0:HP, :, 0:D2]
                    for c in range(2):
                        rows = slice(c * SEQ, (c + 1) * SEQ)
                        for b in range(GB // 2):
                            last = nc.vector.tensor_tensor(to[rows, b, :, c, :], bank[rows, b, :, c, :],
                                                           bias[rows, :, c, :], ALU.add)
                    last.then_inc(bank_free[s.bank(name)], 1)

            def out2(s, p):
                dve.wait_ge(bank_full[s.bank(f"o2{p}")], s.full(f"o2{p}"))
                bank = shared[s.bank(f"o2{p}")][:, 0:HP * PER_TILE * 2 * (D2 + 1)].rearrange(
                    "p (h b c d) -> p h b c d", h=HP, b=PER_TILE, c=2)
                inv = inv2[:, p % 2].rearrange("p (h c) -> p h c", h=HP)
                to = o2[:, p, :].rearrange("p (h c d) -> p h c d", h=HP, c=2)
                for b in range(PER_TILE):
                    rows = slice(b * SEQ, (b + 1) * SEQ)
                    last = nc.vector.reciprocal(inv[rows], bank[rows, :, b, :, D2])
                step(last)
                for b in range(PER_TILE):
                    rows = slice(b * SEQ, (b + 1) * SEQ)
                    last = nc.vector.tensor_tensor(to[rows], bank[rows, :, b, :, 0:D2],
                                                   inv[rows][:, :, :, None].to_broadcast([SEQ, HP, 2, D2]), ALU.mult)
                last.then_inc(bank_free[s.bank(f"o2{p}")], 1)

            def gated(s, p):
                dve.wait_ge(tanh_done, s.item1(p) + 1)
                fg, fh = s.bank(f"fg{p}"), s.bank(f"fh{p}")
                ins = nc.vector.scalar_tensor_tensor(out=tanh_g[:], in0=tanh_g[:], scalar=1.0,
                                                     in1=shared[fg][:], op0=ALU.add, op1=ALU.mult)
                ins.then_inc(bank_free[fg], 1)
                wait_read(dve, s, f"fg{p}")
                dve.wait_ge(bank_full[fh], s.full(f"fh{p}"))
                ins = nc.vector.tensor_tensor(ffT[:, p, :], tanh_g[:], shared[fh][:], ALU.mult)
                ins.then_inc(bank_free[fh], 1)

            def choose(s):
                dve.wait_ge(logits_full, s.g - 1)
                step(nc.vector.tensor_tensor(
                    logits[:], side_router[:, 0:TILES * EXPERTS].rearrange("p (t e) -> p t e", t=TILES),
                    gb_s[:, None, :].to_broadcast([P, TILES, EXPERTS]), ALU.add))
                over = lmax[:, :, None].to_broadcast([P, TILES, EXPERTS])
                step(nc.vector.reduce_max(lmax[:], logits[:], AX_X))
                step(nc.vector.tensor_tensor(chosen, logits[:], over, ALU.is_equal))
                step(nc.vector.tensor_tensor(chosen, chosen, first_wins[:, None, :].to_broadcast([P, TILES, EXPERTS]),
                                             ALU.mult))
                step(nc.vector.reduce_max(lmax[:], chosen, AX_X))
                nc.vector.tensor_tensor(chosen, chosen, over, ALU.is_equal).then_inc(chosen_ready, 1)

            def positions(s):
                dve.wait_ge(ranks_read, s.g - 1)
                dve.wait_ge(chosen_ready, s.g - 1)
                for t in range(TILES):
                    step(nc.vector.tensor_tensor(next_at[:, t + 1], next_at[:, t], rank_count[:, 1, t], ALU.add))
                step(nc.vector.tensor_tensor(spots[:], next_at[:, 0:TILES], rank_count[:, 0], ALU.add))
                step(nc.vector.tensor_tensor(spots[:], spots[:], chosen, ALU.mult))
                step(nc.vector.reduce_sum(position[:], spots[:], AX_X))
                nc.vector.tensor_copy(position_i[:], position[:]).then_inc(positions_ready, 1)
                step(nc.vector.tensor_copy(next_at[:, 0], next_at[:, TILES]))

            def body(s):
                if not (s.attn1 or s.attn2):
                    choose(s)
                    positions(s)
                    return
                if s.attn2:
                    g = s.g - 1
                    dve.wait_ge(bank_full[s.bank("Y")], s.full("Y"))
                    ins = nc.vector.tensor_tensor(x1[:], group_rows(x_s, g),
                                                  shared[s.bank("Y")][:].rearrange("p (t d) -> p t d", t=TILES),
                                                  ALU.add)
                    ins.then_inc(bank_free[s.bank("Y")], 1)
                    wait_read(dve, s, "Y")
                    statistics("rows", tiles_in(x1), var_ready, 3 * g + 1)
                    if s.route:
                        choose(s)
                    step(normed(x1, z, 3 * g + 1))
                    norm(z, hn, 3 * g + 2).then_inc(hn_ready, 1)
                    dve.wait_ge(hn_ready, s.g)
                    step(nc.vector.tensor_tensor(z[:], z[:], bo_s[:, None, :].to_broadcast([P, TILES, P]), ALU.add))
                if s.prepare:
                    next_first(s.g + 1)
                for p in range(TILES):
                    if s.attn1:
                        dve.wait_ge(score1_full, s.item1(p) + 1)
                        less_max(score1, max1, prob1, score1_free)
                    if s.attn1 and p:
                        gated(s, p)
                    if s.attn2 and p == 0:
                        values2_in(s)
                    if s.attn1:
                        dve.wait_ge(exp1_done, s.item1(p) + 1)
                        invert_sum(prob1, sum1, inv1, inv1_ready)
                    if s.attn1 and p == 0:
                        gated(s, p)
                    if s.prepare and p == 0:
                        next_shift(2 * TILES, 2 * s.g + 3)
                    if s.attn2:
                        dve.wait_ge(score2_full, s.item2(p) + 1)
                        less_max(score2, max2, prob2, score2_free)
                        if p:
                            out2(s, p - 1)
                if s.prepare:
                    next_second(s.g + 1)
                if s.route:
                    positions(s)
                if s.prepare:
                    next_shift(TILES, 2 * s.g + 4)
                if s.attn2:
                    out2(s, TILES - 1)
                    g = s.g - 1
                    dve.wait_ge(bank_full[s.bank("P")], s.full("P"))
                    ins = nc.vector.tensor_tensor(z[:], z[:], shared[s.bank("P")][:].rearrange(
                        "p (t d) -> p t d", t=TILES), ALU.add)
                    ins.then_inc(bank_free[s.bank("P")], 1)
                    wait_read(dve, s, "P")
                    wait(dve, scattered, 16 * TILES * (s.g - 1))
                    norm(z, rows_out[:, :, RN:RN + P], 3 * g + 3).then_inc(h2_ready, 1)
                    dve.wait_ge(h2_ready, s.g)
                    step(nc.vector.tensor_scalar(rows_out[:, :, RI], rows_out[:, :, RI], float(GT), None, ALU.add))
                    step(nc.vector.tensor_tensor(rows_out[:, :, RT:RT + P], x1[:], z[:], ALU.add))

            body(first_step())
            body(second_step())
            first_end = count["n"]
            per_middle = MIDDLE_VECTOR_STEPS
            with dve.Fori(2, groups - 1) as g:
                count["base"], count["n"] = (g - 2) * per_middle + first_end, 0
                body(middle_step(g))
                assert count["n"] == per_middle, f"MIDDLE_VECTOR_STEPS is {count['n']}"
            count["base"], count["n"] = 0, first_end + (groups - 3) * per_middle
            body(last_step())
            body(drain_step())
            body(route_step())

            nc.vector.tensor_copy(filling_at[:], next_at[:, 0]).then_inc(filling_at_ready, 1)
            step(nc.vector.tensor_tensor(rows_of[:], next_at[:, 0], room_at[:], ALU.subtract))
            step(nc.vector.tensor_tensor(compare[:], starts[:, None, :].to_broadcast([P, EXPERTS, blocks]),
                                         rows_of[:, :, None].to_broadcast([P, EXPERTS, blocks]), ALU.is_lt))
            step(nc.vector.reduce_sum(padded[:], compare[:], AX_X))
            step(nc.vector.tensor_scalar(padded[:], padded[:], float(BLOCK), None, ALU.mult))
            step(nc.vector.tensor_tensor_scan(padded_end[:], ones[:, 0:EXPERTS], padded[:], 0.0, ALU.mult, ALU.add))
            step(nc.vector.tensor_tensor(compare_b[:], padded_end[:, None, :].to_broadcast([P, blocks, EXPERTS]),
                                         starts[:, :, None].to_broadcast([P, blocks, EXPERTS]), ALU.is_le))
            step(nc.vector.tensor_scalar(padded[:], padded[:], -1.0, float(room), ALU.mult, ALU.add))
            step(nc.vector.tensor_tensor(jumps[:], compare_b[:], padded[:, None, :].to_broadcast([P, blocks, EXPERTS]),
                                         ALU.mult))
            step(nc.vector.reduce_sum(block_at[:], jumps[:], AX_X))
            step(nc.vector.tensor_tensor(block_at[:], block_at[:], starts[:], ALU.add))
            step(nc.vector.tensor_scalar(block_at_i[:], block_at[:], float(idle_at), None, ALU.min))
            step(nc.vector.reduce_sum(block_expert[:], compare_b[:], AX_X))
            nc.vector.tensor_scalar(block_expert_i[:], block_expert[:], float(EXPERTS - 1), None,
                                    ALU.min).then_inc(blocks_ready, 1)

            def experts_mid(s, slot, nth):
                w = expert_w[slot]
                dve.wait_ge(block_in[slot], 16 * nth)
                if not (isinstance(s, int) and s < SLOTS):
                    dve.wait_ge(out_stored[slot], 16 * BA * (nth - 1))
                nc.vector.tensor_copy(token_i[:, slot], block_rows[slot][:, :, RI])
                for c in range(FC):
                    if c % 2 == 0:
                        dve.wait_ge(mid_full, 2 * s + c // 2 + 1)
                    nc.vector.tensor_scalar(mid[slot % 2][:, c, :], mid_bank(slot % 2, c), w[:, EB1 + c:EB1 + c + 1],
                                            0.0, ALU.add, ALU.max).then_inc(mid_ready, 1)
                if not (isinstance(s, int) and s == 0):
                    output(s - 1, (slot - 1) % SLOTS)

            def output(s, slot):
                dve.wait_ge(rest_ready, s + 1)
                dve.wait_ge(y_full, s + 1)
                nc.vector.tensor_tensor(y_rows[slot], y_bank(slot).rearrange("p (a d) -> p a d", a=BA),
                                        block_rows[slot][:, :, RT:RT + P], ALU.add).then_inc(y_ready, 1)

            for_blocks(dve, experts_mid)
            output(blocks - 1, (blocks - 1) % SLOTS)

        @block.tensor
        def _(pe):
            def claim(s, name):
                b = s.bank(name)
                wait(pe, bank_free[b], s.full(name) - 1)
                return shared[b]

            def done(s, name, ins):
                ins.then_inc(bank_full[s.bank(name)], 1)

            def turn(bank, rows):
                for t in range(TILES):
                    last = nc.tensor.transpose(bank[:, t * P:(t + 1) * P], rows[:, t, :], ident[:])
                return last

            def mm(to, lhsT, rhs, start=True, stop=True):
                return nc.tensor.matmul(to, lhsT, rhs, start=start, stop=stop)

            def rows_twice(to, T, b, w):
                for half in range(2):
                    last = mm(to[half * SEQ:(half + 1) * SEQ], T[:, b * SEQ:(b + 1) * SEQ], w)
                return last

            def scores1(s, p):
                wait(pe, score1_free, s.item1(p))
                for h in range(HP):
                    if p == 0 and h >= HP - 2:
                        wait_read(pe, s, f"Q{h}")
                    for b in range(PER_TILE):
                        at = p * P + b * SEQ
                        last = mm(score1[b * SEQ:(b + 1) * SEQ, 2 * h:2 * h + 2, :], qT[:, h, at:at + SEQ],
                                  kblock[:, PER_TILE * p + b])
                last.then_inc(score1_full, 1)

            def scores2(s, p):
                wait(pe, score2_free, s.item2(p))
                pe.wait_ge(spread_ready, s.item2(p) + 1)
                for half in range(2):
                    for b in range(PER_TILE):
                        at = p * P + b * SEQ
                        hs = slice(half * HEADS // 2, (half + 1) * HEADS // 2)
                        last = mm(score2[b * SEQ:(b + 1) * SEQ, hs, :], q2T[:, at:at + SEQ],
                                  kspread[:, p % 2, b, hs, :])
                last.then_inc(score2_full, 1)

            def turn_probs(which, s, p):
                prob, ready, item = (prob1, prob1_ready, s.item1(p)) if which == "1" else \
                    (prob2, exp2_done, s.item2(p))
                pe.wait_ge(ready, item + 1)
                wait(pe, tr_free, tr_index(s, which, p))
                for h in range(HP):
                    last = nc.tensor.transpose(transposed[:, h, :], prob[:, 2 * h:2 * h + 2, :], ident[:])
                last.then_inc(tr_full, 1)

            def values1(s, p):
                pe.wait_ge(tr_free, tr_index(s, "1", p) + 1)
                for b in range(PER_TILE):
                    name = f"o1{'ab'[b]}{p}"
                    bank = claim(s, name)
                    done(s, name, mm(bank[:], vblock[:, PER_TILE * p + b], pT1[:, :, b * SEQ:(b + 1) * SEQ]))

            def values2(s, p):
                pe.wait_ge(tr_free, tr_index(s, "2", p) + 1)
                bank = claim(s, f"o2{p}")
                own = PER_TILE * 2 * (D2 + 1)
                for h in range(HP):
                    last = mm(bank[:, h * own:(h + PAIRS) * own], pT2[:, h, :],
                              v2block[:, PER_TILE * p:PER_TILE * (p + 1), h:h + PAIRS].rearrange(
                                  "p b h c d -> p h b (c d)"))
                done(s, f"o2{p}", last)

            pe.wait_ge(const_ready, 1)
            pe.wait_ge(next_rows, 2)
            for b, rows in enumerate((xh, ch)):
                turn(shared[b], rows).then_inc(bank_full[b], 1)
            pe.wait_ge(weights_in, WEIGHTS_IN)
            pe.wait_ge(half_w, 1)

            def body(s):
                def ranks():
                    pe.wait_ge(chosen_ready, s.g - 1)
                    mm(side_router[:, 0:WIDE], below[:], chosen_wide[:])
                    mm(side_router[:, WIDE:2 * WIDE], ones[:, 0:P], chosen_wide[:]).then_inc(ranks_full, 1)

                if s.attn2:
                    if not s.attn1:
                        for b in range(2):
                            pe.wait_ge(bank_free[b], s.used[b])
                    pe.wait_ge(y1_read, s.g)
                    done(s, "Y", turn(claim(s, "Y"), yT[:].rearrange("p (t d) -> p t d", t=TILES)))
                if s.attn1:
                    for b in range(2):
                        pe.wait_ge(bank_free[b], s.used[b])
                    done(s, "K", mm(claim(s, "K")[:], wk1_s[:].rearrange("p a d -> p (a d)"), cnT[:]))
                    bank = claim(s, "V")
                    for b in range(GB):
                        last = rows_twice(bank[:, b * D1:(b + 1) * D1], cnT, b, wv1_s[:])
                    done(s, "V", last)
                    for h in range(HP):
                        if s.route and h == RANKS_AT:
                            ranks()
                        done(s, f"Q{h}", mm(claim(s, f"Q{h}")[:], wq1_s[:, h * P:(h + 1) * P], xnT[:]))
                elif s.route:
                    ranks()
                if not (s.attn1 or s.attn2):
                    pe.wait_ge(ranks_read, s.g - 1)
                    return
                if s.attn2:
                    pe.wait_ge(hn_ready, s.g)
                    done(s, "H", turn(claim(s, "H"), hn))
                if s.attn1 and s.attn2:
                    pe.wait_ge(y1_read, s.g)
                if s.attn1 and s.route:
                    pe.wait_ge(ranks_read, s.g - 1)

                def project2():
                    wait_read(pe, s, "H")
                    done(s, "k2", mm(claim(s, "k2")[:], wk2_s[:], hnT[:]))
                    done(s, "q2", mm(claim(s, "q2")[:], wq2_s[:], hnT[:]))
                    for half, name in enumerate(("v2a", "v2b")):
                        bank = claim(s, name)
                        for b in range(GB // 2):
                            last = rows_twice(bank[:, b * P:(b + 1) * P], hnT, half * GB // 2 + b, wv2_s[:])
                        done(s, name, last)

                for p in range(TILES):
                    if s.attn1:
                        scores1(s, p)
                    if s.attn2 and p == 0:
                        project2()
                    if s.attn1:
                        for name, at in ((f"fg{p}", FF), (f"fh{p}", 0)):
                            done(s, name, mm(claim(s, name)[:], wff1_s[:, at + p * P:at + (p + 1) * P], xnT[:]))
                    if s.attn2 and p:
                        turn_probs("2", s, p - 1)
                    if s.attn2:
                        if p == 0:
                            for name in ("v2a", "v2b"):
                                wait_read(pe, s, name)
                        scores2(s, p)
                    if s.attn1 and p:
                        values1(s, p - 1)
                    if s.attn2 and p:
                        values2(s, p - 1)
                    if s.attn1:
                        turn_probs("1", s, p)
                def w_part(chunks):
                    if s.attn1:
                        for c in chunks:
                            lhsT, rhs = (wff2_s[:, c, :], ffT[:, c, :]) if c < FC else \
                                (wo1_s[:, c - FC, :], oT[:, c - FC, :])
                            last = mm(side_y, lhsT, rhs, start=(c == 0), stop=(c == FC + HP - 1))
                        if chunks[-1] == FC + HP - 1:
                            last.then_inc(y1_full, 1)

                if s.attn1:
                    pe.wait_ge(score1_free, s.item1(TILES))
                    wait_read(pe, s, f"fh{TILES - 1}")
                w_part(range(0, FC))
                if s.attn2:
                    turn_probs("2", s, TILES - 1)
                if s.attn1:
                    values1(s, TILES - 1)
                if s.attn2:
                    values2(s, TILES - 1)
                if s.attn1:
                    for name in (f"o1a{TILES - 1}", f"o1b{TILES - 1}"):
                        wait_read(pe, s, name)
                w_part(range(FC, FC + 2))
                if s.attn2:
                    wait_read(pe, s, f"o2{TILES - 1}")
                    done(s, "O", turn(claim(s, "O"), o2))
                w_part(range(FC + 2, FC + 3))
                if s.attn2:
                    wait_read(pe, s, "O")
                    bank = claim(s, "P")
                    for t in range(TILES):
                        last = mm(bank[:, t * P:(t + 1) * P], o2T[:, t * P:(t + 1) * P], wo2_s[:])
                    done(s, "P", last)
                w_part(range(FC + 3, FC + HP))
                if s.prepare:
                    pe.wait_ge(next_rows, 2 * s.g + 4)
                    done(s, "X", turn(claim(s, "X"), xh))
                if s.attn2:
                    pe.wait_ge(h2_ready, s.g)
                    done(s, "G", turn(claim(s, "G"), rows_out[:, :, RN:RN + P]))
                if s.prepare:
                    done(s, "C", turn(claim(s, "C"), ch))
                if s.attn2:
                    wait_read(pe, s, "G")
                    if s.route:
                        pe.wait_ge(ranks_read, s.g - 1)
                    for t in range(TILES):
                        last = mm(side_router[:, t * EXPERTS:t * EXPERTS + WIDE], h2T[:, t * P:(t + 1) * P], gw_s[:])
                    last.then_inc(logits_full, 1)

            run_pipeline(pe, body)

            def turn_block(s, slot, nth):
                pe.wait_ge(block_in[slot], 16 * nth)
                wait(pe, block_T, s - 1)
                for a in range(BA):
                    last = nc.tensor.transpose(turned_bank(slot)[:, a * P:(a + 1) * P], block_rows[slot][:, a, RN:RN + P],
                                               ident[:])
                last.then_inc(block_turned, 1)

            def output(s, slot):
                wait(pe, y_ready, s - 1)
                w = expert_w[slot]
                for a in range(BA):
                    for c in range(FC):
                        if a == 0:
                            pe.wait_ge(mid_ready, FC * s + c + 1)
                        last = mm(y_bank(slot)[:, a * P:(a + 1) * P], mid[slot % 2][:, c, a * P:(a + 1) * P],
                                  w[:, EW2 + c * P:EW2 + (c + 1) * P], start=(c == 0), stop=(c == FC - 1))
                last.then_inc(y_full, 1)

            def one_block(s, slot, nth):
                if not (isinstance(s, int) and s == blocks - 1):
                    turn_block(s + 1, (slot + 1) % SLOTS, nth + (slot + 1) // SLOTS)
                pe.wait_ge(expert_w_ready, s + 1)
                pe.wait_ge(block_T, s + 1)
                wait(pe, mid_ready, FC * (s - 1))
                w = expert_w[slot]
                for c in range(FC):
                    last = mm(mid_bank(slot % 2, c), w[:, EW1 + c * P:EW1 + (c + 1) * P], blockT[slot % 2])
                    if c % 2:
                        last.then_inc(mid_full, 1)
                if not (isinstance(s, int) and s == 0):
                    output(s - 1, (slot - 1) % SLOTS)

            turn_block(0, 0, 1)
            for_blocks(pe, one_block)
            output(blocks - 1, (blocks - 1) % SLOTS)


def kernel(**inputs):
    import numpy as np

    import concourse.bacc as bacc
    from concourse.bass_utils import run_bass_kernel_spmd

    a = {k: np.asarray(v) for k, v in inputs.items()}
    f = {k[len("L0_ffn_"):]: v for k, v in a.items() if k.startswith("L0_ffn_")}
    c = {k[len("L0_xattn_"):]: v for k, v in a.items() if k.startswith("L0_xattn_")}
    shape = a["x"].shape
    width = shape[-1]
    w2 = f["w2"].reshape(EXPERTS, FC, P, P).transpose(0, 2, 1, 3).reshape(EXPERTS, P, FC * P)
    b1 = f["b1"].reshape(EXPERTS, FC, P).transpose(0, 2, 1)
    b2 = np.broadcast_to(f["b2"][:, None, :], (EXPERTS, P, P))
    experts = np.concatenate([f["w1"], w2, b1, b2], axis=2)
    laid = {
        "x": a["x"].reshape(-1, width), "ctx": a["ctx_1024"].reshape(-1, width),
        "wq1": c["Wq"], "wk1": c["Wkv"][:, :D1], "wv1": c["Wkv"][:, D1:], "wo1": c["Wo"],
        "wff1": c["Wff1"], "wff2": c["Wff2"], "wq2": f["wq"], "wk2": f["wk"], "wv2": f["wv"], "wo2": f["wo"],
        "vectors": np.stack([c["ln_g"], c["ln_b"], c["cln_g"], c["cln_b"], f["ln1_g"], f["ln1_b"], f["ln2_g"],
                             f["ln2_b"], f["bq"], f["bk"]], axis=1),
        "bv": f["bv"], "bo": f["bo"], "gate_w": f["gate_w"], "gate_b": f["gate_b"], "experts": experts,
    }
    nc = bacc.Bacc("TRN2", target_bir_lowering=False, num_devices=1)
    arrays, args = {}, []
    for name, v in laid.items():
        v = np.ascontiguousarray(v)
        arrays[f"in_{name}"] = v
        args.append(nc.dram_tensor(f"in_{name}", v.shape, mybir.dt.from_np(v.dtype), kind="ExternalInput").ap())
    args.append(nc.dram_tensor("out_x", arrays["in_x"].shape, F32, kind="ExternalOutput").ap())
    build(nc, *args)
    r = run_bass_kernel_spmd(nc, [arrays], core_ids=[0])
    return r.results[0]["out_x"].reshape(shape)
```

```python
from contextlib import ExitStack

import concourse.bass as bass
from concourse import mybir
from concourse.alu_op_type import AluOpType as ALU

F32 = mybir.dt.float32
F32R = mybir.dt.float32r
I32 = mybir.dt.int32
ACT = mybir.ActivationFunctionType
AX_X = mybir.AxisListType.X

P = 128
SEQ = 64
PER_TILE = P // SEQ
TILES = 4
GT = TILES * P
GB = GT // SEQ
HEADS = 16
HP = HEADS // 2
D1 = 64
D2 = P // HEADS
FF = 512
FC = FF // P
EXPERTS = 8
BLOCK = 128
BA = BLOCK // P
WIDE = 128
PAIRS = 3
EPS = 1e-5
SCALE1 = float(D1) ** -0.5
SCALE2 = float(D2) ** -0.5
LN_G, LN_B, CLN_G, CLN_B, LN1_G, LN1_B, LN2_G, LN2_B, BQ, BK = range(10)
EW1, EW2, EB1, EB2, EN = 0, FF, FF + FC * P, FF + FC * P + FC, FF + FC * P + FC + P
RN, RT, RI, ROW = 0, P, 2 * P, 2 * P + 1
RANKS_AT = 5
SLOTS = 6


def psum_uses(attn1, attn2, prepare):
    uses = []
    if attn2:
        uses += ["Y"]
    if attn1:
        uses += ["K", "V"]
        if not attn2:
            uses += ["X0"]
        uses += [f"Q{h}" for h in range(HP)]
    if attn2:
        uses += ["H"]
    for p in range(TILES):
        if attn2 and p == 0:
            uses += ["k2", "q2", "v2a", "v2b"]
        if attn1:
            uses += [f"fg{p}", f"fh{p}"]
        if attn1 and p:
            uses += [f"o1a{p - 1}", f"o1b{p - 1}"]
        if attn2 and p:
            uses += [f"o2{p - 1}"]
    if attn1:
        uses += [f"o1a{TILES - 1}", f"o1b{TILES - 1}"]
    if attn2:
        uses += [f"o2{TILES - 1}", "O", "P"]
    if prepare:
        uses += ["X"]
    if attn2:
        uses += ["G"]
    if prepare:
        uses += ["C"]
    return [(name, at % 2) for at, name in enumerate(uses)]


MIDDLE_VECTOR_STEPS = 44


class Step:

    def __init__(self, g, attn1, attn2, prepare, route, before):
        self.g, self.attn1, self.attn2, self.prepare, self.route = g, attn1, attn2, prepare, route
        self.uses = psum_uses(attn1, attn2, prepare)
        self.used = [before(0), before(1)]

    def bank(self, name):
        return dict(self.uses)[name]

    def full(self, name):
        bank = self.bank(name)
        return self.used[bank] + [n for n, b in self.uses if b == bank].index(name) + 1

    def item1(self, p):
        return TILES * self.g + p

    def item2(self, p):
        return TILES * (self.g - 1) + p


def wait(engine, semaphore, value):
    if isinstance(value, int) and value <= 0:
        return
    engine.wait_ge(semaphore, value)


def build(nc, x, ctx_in, wq1, wk1, wv1, wo1, wff1, wff2, wq2, wk2, wv2, wo2, vectors, bv, bo, gate_w,
          gate_b, experts, out):
    tokens = x.shape[0]
    groups = tokens // GT
    tiles = tokens // P
    blocks = tokens // BLOCK + EXPERTS - 1
    room = tokens + BLOCK
    idle_at = EXPERTS * room

    sorted_in = nc.dram_tensor("sorted_in", [idle_at + BLOCK, ROW], F32, kind="Internal").ap()

    es = ExitStack()
    with es:
        def sb(name, shape, dt=F32):
            return es.enter_context(nc.sbuf_tensor(name, shape, dt))

        def ps(name, shape):
            return es.enter_context(nc.psum_tensor(name, shape, F32))

        def sem(name):
            return es.enter_context(nc.semaphore(name))

        wq1_hi, wq1_lo = sb("wq1_hi", [P, HEADS * D1], F32R), sb("wq1_lo", [P, HEADS * D1], F32R)
        wff1_hi, wff1_lo = sb("wff1_hi", [P, 2 * FF], F32R), sb("wff1_lo", [P, 2 * FF], F32R)
        wk1_s = sb("wk1_s", [P, 2, D1])
        wv1_s = sb("wv1_s", [P, D1])
        wo1_s = sb("wo1_s", [P, HP, P])
        wff2_s = sb("wff2_s", [P, FC, P])
        wq2_s = sb("wq2_s", [P, P])
        wk2_s = sb("wk2_s", [P, P])
        wv2_s = sb("wv2_s", [P, P])
        wo2_s = sb("wo2_s", [P, P])
        vec = sb("vec", [P, 10])
        bv_s = sb("bv_s", [P, P])
        bo_s = sb("bo_s", [P, P])
        gw_s = sb("gw_s", [P, WIDE])
        gb_s = sb("gb_s", [P, EXPERTS])
        ident = sb("ident", [P, P])
        head_mask = sb("head_mask", [P, HEADS])
        below = sb("below", [P, P])
        ones = sb("ones", [P, 256])
        first_wins = sb("first_wins", [P, EXPERTS])
        starts = sb("starts", [P, blocks])
        room_at = sb("room_at", [P, EXPERTS])
        filling = sb("filling", [P, BA, ROW])
        ints = sb("ints", [P, EXPERTS + blocks], I32)
        ints_at = sb("ints_at", [P, EXPERTS], I32)
        ints_id = sb("ints_id", [P, TILES + BA], I32)

        x_s = sb("x_s", [P, tiles, P])
        expert_all = sb("expert_all", [P, EXPERTS, EN])
        c_s = expert_all[:].rearrange("p e n -> p (e n)")[:, 0:tiles * P].rearrange("p (t d) -> p t d", t=tiles)
        apart = -(-tiles * P // EN)

        xh = sb("xh", [P, TILES, P])
        ch = sb("ch", [P, TILES, P])
        xnT = sb("xnT", [P, GT])
        xnT_hi, xnT_lo = sb("xnT_hi", [P, GT], F32R), sb("xnT_lo", [P, GT], F32R)
        cnT = sb("cnT", [P, GT])
        kblock = sb("kblock", [P, GB, 2, SEQ])
        vblock = sb("vblock", [P, GB, 2, D1])
        qT = sb("qT", [P, HP, GT])
        oT = sb("oT", [P, HP, GT])
        tanh_g = sb("tanh_g", [P, GT])
        ffT = sb("ffT", [P, FC, GT])
        prob1 = sb("prob1", [P, HEADS, SEQ])
        prob2 = sb("prob2", [P, HEADS, SEQ])
        pT1 = sb("pT1", [P, HP, P])
        pT2 = sb("pT2", [P, HP, P])
        yT = sb("yT", [P, GT])
        x1 = sb("x1", [P, TILES, P])
        z = sb("z", [P, TILES, P])
        hn = sb("hn", [P, TILES, P])
        hnT = sb("hnT", [P, GT])
        q2T = sb("q2T", [P, GT])
        k2T = sb("k2T", [P, GT])
        v2block = sb("v2block", [P, GB, HP + PAIRS - 1, 2, D2 + 1])
        kspread = sb("kspread", [P, 2, PER_TILE, HEADS, SEQ])
        wq1_s, wff1_s = (kspread[:].rearrange("p a b h j -> p (a b h j)")[:, i * 2 * FF:(i + 1) * 2 * FF]
                         for i in range(2))
        o2 = sb("o2", [P, TILES, P])
        o2T = q2T
        h2T = hnT
        max1 = sb("max1", [P, 2, HEADS])
        max2 = sb("max2", [P, 2, HEADS])
        sum1 = sb("sum1", [P, HEADS])
        inv1 = sb("inv1", [P, 2, HEADS])
        inv2 = sb("inv2", [P, 2, HEADS])
        rows_out = sb("rows_out", [P, TILES, ROW])
        logits = sb("logits", [P, TILES, EXPERTS])
        chosen_wide = sb("chosen_wide", [P, WIDE])
        chosen = chosen_wide[:, 0:TILES * EXPERTS].rearrange("p (t e) -> p t e", t=TILES)
        lmax = sb("lmax", [P, TILES])
        rank_count = sb("rank_count", [P, 2, TILES, EXPERTS])
        next_at = sb("next_at", [P, TILES + 1, EXPERTS])
        spots = sb("spots", [P, TILES, EXPERTS])
        position = sb("position", [P, TILES])
        position_i = sb("position_i", [P, TILES], I32)
        filling_at = sb("filling_at", [P, EXPERTS], I32)
        rows_of = sb("rows_of", [P, EXPERTS])
        padded = sb("padded", [P, EXPERTS])
        padded_end = sb("padded_end", [P, EXPERTS])
        compare, compare_b, jumps = (
            ffT[:].rearrange("p c t -> p (c t)")[:, i * EXPERTS * blocks:(i + 1) * EXPERTS * blocks].rearrange(
                "p (a b) -> p a b", a=a) for i, a in enumerate((EXPERTS, blocks, blocks)))
        block_expert = sb("block_expert", [P, blocks])
        block_expert_i = sb("block_expert_i", [P, blocks], I32)
        block_at = sb("block_at", [P, blocks])
        block_at_i = sb("block_at_i", [P, blocks], I32)
        token_i = sb("token_i", [P, SLOTS, BA], I32)
        stat, mv, var, rstd, shift_n = ({which: sb(f"{name}_{which}", [P, n] + rest)
                                         for which, n in (("rows", TILES), ("next", 2 * TILES))}
                                        for name, rest in (("stat", [6]), ("mv", [2]), ("var", []), ("rstd", []),
                                                           ("shift", [])))
        minus_half = sb("minus_half", [P, 2 * TILES])
        carrier = sb("carrier", [P, 1])

        def from_buffer(buffer, at, shape):
            names = "abcd"[:len(buffer.shape) - 1]
            flat = buffer[:].rearrange(f"p {' '.join(names)} -> p ({' '.join(names)})")
            if len(shape) == 1:
                return flat[:, at:at + shape[0]]
            return flat[:, at:at + shape[0] * shape[1]].rearrange("p (a b) -> p a b", a=shape[0])

        expert_w = [from_buffer(buffer, i * EN, [EN]) for buffer in (oT, kspread) for i in range(SLOTS // 2)]
        block_rows = [from_buffer(qT, i * BA * ROW, [BA, ROW]) for i in range(SLOTS)]
        y_rows = [from_buffer(qT, SLOTS * BA * ROW + i * BLOCK, [BA, P]) for i in range(SLOTS)]
        blockT = [from_buffer(kspread, SLOTS // 2 * EN + i * BLOCK, [BLOCK]) for i in range(2)]
        mid = [from_buffer(ffT, i * FC * BLOCK, [FC, BLOCK]) for i in range(2)]

        score1 = ps("score1", [P, HEADS, SEQ])
        score2 = ps("score2", [P, HEADS, SEQ])
        transposed = ps("transposed", [P, HP, P])
        shared = [ps(f"shared{i}", [P, GT]) for i in range(2)]
        side_y, side_router = (score1[:].rearrange("p h j -> p (h j)")[:, b * GT:(b + 1) * GT] for b in range(2))

        context_in = sem("context_in")
        queries_in = sem("queries_in")
        weights_in = sem("weights_in")
        weights_split = sem("weights_split")
        xnT_lo_ready = sem("xnT_lo_ready")
        hi_done = sem("hi_done")
        rows0_in = sem("rows0_in")
        rows_in = sem("rows_in")
        filled = sem("filled")
        const_step = sem("const_step")
        const_ready = sem("const_ready")
        half_ready = sem("half_ready")
        half_w = sem("half_w")
        var_ready = sem("var_ready")
        rstd_ready = sem("rstd_ready")
        next_var_ready = sem("next_var_ready")
        next_rstd_ready = sem("next_rstd_ready")
        next_shift_ready = sem("next_shift_ready")
        x_once = sem("x_once")
        next_rows = sem("next_rows")
        dve_done = sem("dve_done")
        bank_full = [sem(f"bank_full{i}") for i in range(2)]
        bank_free = [sem(f"bank_free{i}") for i in range(2)]
        score1_full = sem("score1_full")
        score1_free = sem("score1_free")
        exp1_done = sem("exp1_done")
        inv1_ready = sem("inv1_ready")
        prob1_ready = sem("prob1_ready")
        score2_full = sem("score2_full")
        score2_free = sem("score2_free")
        exp2_done = sem("exp2_done")
        tr_full = sem("tr_full")
        tr_free = sem("tr_free")
        tanh_done = sem("tanh_done")
        hn_ready = sem("hn_ready")
        spread_ready = sem("spread_ready")
        h2_ready = sem("h2_ready")
        y1_full = sem("y1_full")
        y1_read = sem("y1_read")
        logits_full = sem("logits_full")
        chosen_ready = sem("chosen_ready")
        ranks_full = sem("ranks_full")
        ranks_read = sem("ranks_read")
        positions_ready = sem("positions_ready")
        filling_at_ready = sem("filling_at_ready")
        blocks_ready = sem("blocks_ready")
        scattered = sem("scattered")
        experts_in = sem("experts_in")
        block_in = [sem(f"block_in{i}") for i in range(SLOTS)]
        block_turned = sem("block_turned")
        block_T = sem("block_T")
        expert_w_ready = sem("expert_w_ready")
        mid_full = sem("mid_full")
        mid_ready = sem("mid_ready")
        y_full = sem("y_full")
        rest_ready = sem("rest_ready")
        y_ready = sem("y_ready")
        out_stored = [sem(f"out_stored{i}") for i in range(SLOTS)]

        FIRST = dict(attn1=True, attn2=False, prepare=True, route=False)
        SECOND = dict(attn1=True, attn2=True, prepare=True, route=False)
        MID = dict(attn1=True, attn2=True, prepare=True, route=True)
        LAST = dict(attn1=True, attn2=True, prepare=False, route=True)
        DRAIN = dict(attn1=False, attn2=True, prepare=False, route=True)
        ROUTE = dict(attn1=False, attn2=False, prepare=False, route=True)

        def in_bank(kind, b):
            return sum(bank == b for _, bank in psum_uses(kind["attn1"], kind["attn2"], kind["prepare"]))

        def first_step():
            return Step(0, before=lambda b: b, **FIRST)

        def second_step():
            return Step(1, before=lambda b: b + in_bank(FIRST, b), **SECOND)

        def at_middle(g, b):
            return b + in_bank(FIRST, b) + in_bank(SECOND, b) + (g - 2) * in_bank(MID, b)

        def middle_step(g):
            return Step(g, before=lambda b: at_middle(g, b), **MID)

        def last_step():
            return Step(groups - 1, before=lambda b: at_middle(groups - 1, b), **LAST)

        def drain_step():
            return Step(groups, before=lambda b: at_middle(groups - 1, b) + in_bank(LAST, b), **DRAIN)

        def route_step():
            return Step(groups + 1, before=lambda b: at_middle(groups - 1, b) + in_bank(LAST, b)
                        + in_bank(DRAIN, b), **ROUTE)

        def wait_read(engine, s, name):
            engine.wait_ge(bank_free[s.bank(name)], s.full(name))

        def group_rows(rows, g):
            return rows[:, bass.ds(g * TILES, TILES), :] if not isinstance(g, int) else \
                rows[:, g * TILES:(g + 1) * TILES, :]

        def run_pipeline(engine, body):
            body(first_step())
            body(second_step())
            with engine.Fori(2, groups - 1) as g:
                body(middle_step(g))
            body(last_step())
            body(drain_step())
            body(route_step())

        def buffers(s, which, p):
            own = int(which) - 1
            if not (s.attn1 and s.attn2) and p % 2:
                own = 1 - own
            return ((score1, prob1), (score2, prob2))[own]

        def transposes_before(s):
            if isinstance(s.g, int) and s.g == 0:
                return 0
            return TILES + (s.g - 1) * 2 * TILES

        tr_order = {}
        for kind, (a1, a2) in (("first", (True, False)), ("mid", (True, True)), ("drain", (False, True))):
            order = []
            for p in range(TILES):
                if a2 and p:
                    order.append(("2", p - 1))
                if a1:
                    order.append(("1", p))
            if a2:
                order.append(("2", TILES - 1))
            tr_order[(a1, a2)] = order

        def tr_index(s, which, p):
            return transposes_before(s) + tr_order[(s.attn1, s.attn2)].index((which, p))

        def mid_bank(slot, c):
            at = c // 2 * GT + c % 2 * BLOCK
            return (score1, score2)[slot][:].rearrange("p h j -> p (h j)")[:, at:at + BLOCK]

        def turned_bank(slot):
            return transposed[:].rearrange("p h c -> p (h c)")[:, slot % 2 * GT:slot % 2 * GT + BLOCK]

        def y_bank(slot):
            return shared[slot % 2][:, 0:BLOCK]

        block = es.enter_context(nc.Block())

        WEIGHTS_IN = 16 * 10
        CONTEXT_IN = 16 * 4

        def for_blocks(engine, run):
            for s in range(SLOTS):
                run(s, s, 1)
            with engine.Fori(1, blocks // SLOTS) as i:
                for slot in range(SLOTS):
                    run(SLOTS * i + slot, slot, i + 1)
            for s in range(blocks // SLOTS * SLOTS, blocks):
                run(s, s % SLOTS, s // SLOTS + 1)

        def put_filling(engine, some):
            engine.wait_ge(filling_at_ready, 1)
            for e in some:
                at = engine.value_load(filling_at[0:1, e:e + 1], min_val=0, max_val=idle_at - BLOCK)
                engine.dma_start(sorted_in[bass.ds(at, BLOCK), :].rearrange("(p a) d -> p a d", p=P),
                                 filling[:]).then_inc(filled, 16)

        @block.sync
        def _(sp):
            xv = x.rearrange("(t p) d -> p t d", p=P)
            cv = ctx_in.rearrange("(t p) d -> p t d", p=P)
            sp.dma_start(x_s[:, 0:TILES, :], xv[:, 0:TILES, :]).then_inc(rows0_in, 16)
            sp.dma_start(c_s[:, 0:TILES, :], cv[:, 0:TILES, :]).then_inc(rows0_in, 16)
            sp.dma_start(vec[:], vectors).then_inc(context_in, 16)
            for half in range(2):
                sp.dma_start(wk1_s[:, half, :], wk1).then_inc(context_in, 16)
            sp.dma_start(wv1_s[:], wv1).then_inc(context_in, 16)
            sp.dma_start(wq1_s, wq1).then_inc(queries_in, 16)
            sp.dma_start(wff1_s, wff1).then_inc(queries_in, 16)
            sp.dma_start(wff2_s[:], wff2.rearrange("(c p) n -> p c n", p=P)).then_inc(weights_in, 16)
            sp.dma_start(wo1_s[:], wo1.rearrange("(c p) n -> p c n", p=P)).then_inc(weights_in, 16)
            for to, of in ((wq2_s, wq2), (wk2_s, wk2), (wv2_s, wv2), (wo2_s, wo2)):
                sp.dma_start(to[:], of).then_inc(weights_in, 16)
            sp.wait_ge(const_ready, 1)
            sp.dma_start(gw_s[:, 0:EXPERTS], gate_w).then_inc(weights_in, 16)
            for to, of in ((bv_s, bv), (bo_s, bo), (gb_s, gate_b)):
                sp.dma_start(to[:], of.partition_broadcast(P)).then_inc(weights_in, 16)
            sp.dma_start(x_s[:, TILES:, :], xv[:, TILES:, :]).then_inc(rows_in, 16)
            sp.dma_start(c_s[:, TILES:, :], cv[:, TILES:, :]).then_inc(rows_in, 16)
            sp.dma_start(sorted_in[idle_at:idle_at + BLOCK, :].rearrange("(p a) d -> p a d", p=P), filling[:]).then_inc(
                filled, 16)
            sp.dma_start(expert_all[:, apart:, :], experts[apart:].rearrange("e p n -> p e n")).then_inc(experts_in, 16)
            sp.wait_ge(next_rows, 2 * groups)
            sp.dma_start(expert_all[:, 0:apart, :], experts[0:apart].rearrange("e p n -> p e n")).then_inc(
                experts_in, 16)

            def load_block(s, slot, nth):
                wait(sp, y_ready, s - SLOTS + 1)
                at = sp.value_load(block_at_i[0:1, bass.ds(s, 1)], min_val=0, max_val=idle_at)
                if isinstance(s, int) and s == 0:
                    sp.wait_ge(scattered, 16 * tiles)
                    sp.wait_ge(filled, 16 * (1 + EXPERTS))
                sp.dma_start(block_rows[slot], sorted_in[bass.ds(at, BLOCK), :].rearrange(
                    "(p a) d -> p a d", p=P)).then_inc(block_in[slot], 16)

            put_filling(sp, range(0, EXPERTS, 2))
            sp.wait_ge(blocks_ready, 1)
            for_blocks(sp, load_block)
            for slot in range(SLOTS):
                sp.wait_ge(out_stored[slot], 16 * BA * len(range(slot, blocks, SLOTS)))

        @block.gpsimd
        def _(pool):
            steps = [0]

            def step(ins):
                steps[0] += 1
                ins.then_inc(const_step, 1)
                pool.wait_ge(const_step, steps[0])

            def inverse_root(which, n, ready, count, done):
                pool.wait_ge(ready, count)
                nc.gpsimd.tensor_tensor(rstd[which][:, 0:n], var[which][:, 0:n], minus_half[:, 0:n],
                                        ALU.pow).then_inc(done, 1)

            nc.gpsimd.memset(minus_half[:], -0.5).then_inc(half_ready, 1)
            nc.gpsimd.memset(ident[:], 0.0)
            nc.gpsimd.memset(head_mask[:], 1.0)
            nc.gpsimd.memset(kblock[:], 0.0)
            nc.gpsimd.memset(vblock[:], 0.0)
            nc.gpsimd.memset(v2block[:], 0.0)
            nc.gpsimd.memset(ones[:], 1.0)
            pool.wait_ge(half_ready, 1)
            inverse_root("next", 2 * TILES, next_var_ready, 1, next_rstd_ready)
            nc.gpsimd.memset(filling[:], 0.0)
            nc.gpsimd.memset(chosen_wide[:], 0.0)
            nc.gpsimd.memset(gw_s[:], 0.0)
            step(nc.gpsimd.memset(below[:], 1.0))
            for c in range(2):
                step(nc.gpsimd.memset(v2block[c * SEQ:(c + 1) * SEQ, :, 0:HP, c, D2:D2 + 1], 1.0))
            step(nc.gpsimd.affine_select(out=ident[:], in_=ident[:], compare_op=ALU.not_equal, fill=1.0,
                                         base=0, pattern=[[-1, P]], channel_multiplier=1))
            step(nc.gpsimd.affine_select(out=head_mask[:], in_=head_mask[:], compare_op=ALU.is_ge, fill=0.0,
                                         base=0, pattern=[[-D2, HEADS]], channel_multiplier=1))
            step(nc.gpsimd.affine_select(out=head_mask[:], in_=head_mask[:], compare_op=ALU.is_ge, fill=0.0,
                                         base=D2 - 1, pattern=[[D2, HEADS]], channel_multiplier=-1))
            step(nc.gpsimd.affine_select(out=below[:], in_=below[:], compare_op=ALU.is_gt, fill=0.0,
                                         base=0, pattern=[[1, P]], channel_multiplier=-1))
            nc.gpsimd.iota(ints[:, 0:EXPERTS], pattern=[[-1, EXPERTS]], base=EXPERTS, channel_multiplier=0)
            nc.gpsimd.iota(ints[:, EXPERTS:], pattern=[[BLOCK, blocks]], base=0, channel_multiplier=0)
            nc.gpsimd.iota(ints_at[:], pattern=[[room, EXPERTS]], base=0, channel_multiplier=0)
            nc.gpsimd.iota(ints_id[:, 0:TILES], pattern=[[P, TILES]], base=-GT, channel_multiplier=1)
            step(nc.gpsimd.iota(ints_id[:, TILES:], pattern=[[1, BA]], base=tokens, channel_multiplier=BA))
            nc.gpsimd.tensor_copy(first_wins[:], ints[:, 0:EXPERTS])
            nc.gpsimd.tensor_copy(starts[:], ints[:, EXPERTS:])
            nc.gpsimd.tensor_copy(room_at[:], ints_at[:])
            nc.gpsimd.tensor_copy(next_at[:, 0, :], ints_at[:])
            nc.gpsimd.tensor_copy(rows_out[:, :, RI], ints_id[:, 0:TILES])
            nc.gpsimd.tensor_copy(filling[:, :, RI], ints_id[:, TILES:]).then_inc(const_ready, 1)

            def spread(s, p):
                for b in range(PER_TILE):
                    at = (PER_TILE * p + b) * SEQ
                    ins = nc.gpsimd.tensor_tensor(
                        kspread[:, p % 2, b], k2T[:, None, at:at + SEQ].to_broadcast([P, HEADS, SEQ]),
                        head_mask[:, :, None].to_broadcast([P, HEADS, SEQ]), ALU.mult)
                ins.then_inc(spread_ready, 1)

            def normalise(s, p):
                prob = buffers(s, "1", p)[1]
                pool.wait_ge(inv1_ready, s.item1(p) + 1)
                nc.gpsimd.tensor_tensor(prob[:], prob[:], inv1[:, p % 2, :, None].to_broadcast([P, HEADS, SEQ]),
                                        ALU.mult).then_inc(prob1_ready, 1)

            inverse_root("next", TILES, next_var_ready, 2, next_rstd_ready)

            def scatter(s):
                for t in range(TILES):
                    nc.gpsimd.indirect_dma_start(
                        out=sorted_in, out_offset=bass.IndirectOffsetOnAxis(ap=position_i[:, t:t + 1], axis=0),
                        in_=rows_out[:, t, :], in_offset=None).then_inc(scattered, 16)

            def body(s):
                if not (s.attn1 or s.attn2):
                    pool.wait_ge(positions_ready, groups)
                    scatter(s)
                    return
                if s.attn2:
                    for turn in (1, 2):
                        inverse_root("rows", TILES, var_ready, 3 * (s.g - 1) + turn, rstd_ready)
                if s.prepare:
                    inverse_root("next", 2 * TILES, next_var_ready, 2 * (s.g + 1) + 1, next_rstd_ready)
                if s.attn2:
                    wait_read(pool, s, "k2")
                    spread(s, 0)
                for p in range(TILES):
                    if s.attn1:
                        normalise(s, p)
                    if s.attn2 and p + 1 < TILES:
                        if p:
                            pool.wait_ge(score2_full, s.item2(p - 1) + 1)
                        spread(s, p + 1)
                if s.prepare:
                    if s.route:
                        pool.wait_ge(positions_ready, s.g - 1)
                    inverse_root("next", TILES, next_var_ready, 2 * (s.g + 1) + 2, next_rstd_ready)
                elif s.route:
                    pool.wait_ge(positions_ready, s.g - 1)
                if s.route:
                    scatter(s)
                if s.attn2:
                    inverse_root("rows", TILES, var_ready, 3 * s.g, rstd_ready)

            run_pipeline(pool, body)

            def block_out(s, slot, nth):
                pool.wait_ge(block_in[slot], 16 * nth)
                pool.wait_ge(expert_w_ready, s + 1)
                wait(pool, y_ready, s)
                rest = block_rows[slot][:, :, RT:RT + P]
                nc.gpsimd.tensor_tensor(rest, rest, expert_w[slot][:, None, EB2:EB2 + P].to_broadcast([P, BA, P]),
                                        ALU.add).then_inc(rest_ready, 1)
                if not (isinstance(s, int) and s == 0):
                    store(s - 1, (slot - 1) % SLOTS)

            def store(s, slot):
                for a in range(BA):
                    nc.gpsimd.indirect_dma_start(
                        out=out, out_offset=bass.IndirectOffsetOnAxis(ap=token_i[:, slot, a:a + 1], axis=0),
                        in_=y_rows[slot][:, a, :], in_offset=None, bounds_check=tokens - 1,
                        oob_is_err=False).then_inc(out_stored[slot], 16)

            for_blocks(pool, block_out)
            pool.wait_ge(y_ready, blocks)
            store(blocks - 1, (blocks - 1) % SLOTS)

        @block.scalar
        def _(act):
            def take(s, name):
                act.wait_ge(bank_full[s.bank(name)], s.full(name))
                return shared[s.bank(name)]

            def affine(to, bank, gain, bias):
                return nc.scalar.activation(to[:], bank[:], ACT.Identity, bias=vec[:, bias:bias + 1],
                                            scale=vec[:, gain:gain + 1])

            def free(s, name, ins):
                ins.then_inc(bank_free[s.bank(name)], 1)

            def copy_out(which, to, s, p):
                act.wait_ge(tr_full, tr_index(s, which, p) + 1)
                nc.scalar.copy(to[:, 0:HP // 2, :], transposed[:, 0:HP // 2, :])
                nc.scalar.copy(to[:, HP // 2:, :], transposed[:, HP // 2:, :]).then_inc(tr_free, 1)

            def out1(s, p):
                for b in range(PER_TILE):
                    bank = take(s, f"o1{'ab'[b]}{p}")
                    at = p * P + b * SEQ
                    free(s, f"o1{'ab'[b]}{p}",
                         nc.scalar.copy(oT[:, :, at:at + SEQ], bank[:].rearrange("p (h i) -> p h i", h=HP)))

            def normed(src, dst, at):
                for t in range(TILES):
                    last = nc.scalar.activation(dst[:, t, :], src[:, t, :], ACT.Identity,
                                                bias=shift_n["next"][:, at + t:at + t + 1],
                                                scale=rstd["next"][:, at + t:at + t + 1])
                return last

            def next_once(g):
                act.wait_ge(next_shift_ready, 2 * g + 1)
                normed(group_rows(x_s, g), xh, 0).then_inc(x_once, 1)

            def next_context(g):
                normed(group_rows(c_s, g), ch, TILES).then_inc(next_rows, 1)

            def next_twice(g):
                act.wait_ge(next_shift_ready, 2 * g + 2)
                normed(xh, xh, 0).then_inc(next_rows, 1)

            next_once(0)
            next_context(0)
            act.wait_ge(context_in, CONTEXT_IN)
            act.wait_ge(const_ready, 1)
            act.wait_ge(bank_full[1], 1)
            affine(cnT, shared[1], CLN_G, CLN_B).then_inc(bank_free[1], 1)
            next_twice(0)

            def tanh(s, p):
                if p:
                    wait_read(act, s, f"fh{p - 1}")
                bank = take(s, f"fg{p}")
                nc.scalar.activation(tanh_g[:], bank[:], ACT.Tanh, scale=0.5).then_inc(tanh_done, 1)

            def route_in(s):
                act.wait_ge(ranks_full, s.g - 1)
                nc.scalar.copy(rank_count[:].rearrange("p w t e -> p w (t e)"), side_router[:, 0:2 * WIDE].rearrange(
                    "p (w n) -> p w n", w=2)[:, :, 0:TILES * EXPERTS]).then_inc(ranks_read, 1)

            def body(s):
                if s.attn1:
                    bank = take(s, "K")[:].rearrange("p (b j) -> p b j", b=GB)
                    nc.scalar.copy(kblock[0:SEQ, :, 0, :], bank[0:SEQ])
                    free(s, "K", nc.scalar.copy(kblock[SEQ:P, :, 1, :], bank[SEQ:P]))
                    bank = take(s, "V")[:].rearrange("p (b j) -> p b j", b=GB)
                    nc.scalar.copy(vblock[0:SEQ, :, 0, :], bank[0:SEQ])
                    free(s, "V", nc.scalar.copy(vblock[SEQ:P, :, 1, :], bank[SEQ:P]))
                    if not s.attn2:
                        free(s, "X0", affine(xnT, take(s, "X0"), LN_G, LN_B))
                if not (s.attn1 or s.attn2):
                    route_in(s)
                    return
                if s.route and not s.attn1:
                    route_in(s)
                if s.attn1:
                    for h in range(HP):
                        if s.route and h == RANKS_AT:
                            route_in(s)
                        free(s, f"Q{h}", nc.scalar.copy(qT[:, h, :], take(s, f"Q{h}")[:]))
                if s.attn2:
                    free(s, "H", affine(hnT, take(s, "H"), LN1_G, LN1_B))
                if s.prepare and not s.attn2:
                    act.wait_ge(rows_in, 32)
                    next_once(s.g + 1)
                    next_context(s.g + 1)
                for p in range(TILES):
                    if s.attn1 and (p or not s.attn2):
                        tanh(s, p)
                    if s.attn2 and p == 0:
                        for name, to, bias in (("k2", k2T, BK), ("q2", q2T, BQ)):
                            free(s, name, nc.scalar.activation(to[:], take(s, name)[:], ACT.Identity,
                                                               bias=vec[:, bias:bias + 1]))
                    if s.attn1:
                        act.wait_ge(score1_free, s.item1(p) + 1)
                        prob = buffers(s, "1", p)[1]
                        nc.scalar.activation(prob[:], prob[:], ACT.Exp, scale=SCALE1).then_inc(exp1_done, 1)
                    if s.attn1 and s.attn2 and p == 0:
                        tanh(s, p)
                        copy_out("1", pT1, s, p)
                    if s.attn1 and not s.attn2 and p:
                        copy_out("1", pT1, s, p - 1)
                    if s.attn1 and s.attn2 and p:
                        copy_out("2", pT2, s, p - 1)
                    if s.attn1 and p:
                        out1(s, p - 1)
                    if s.attn2:
                        act.wait_ge(score2_free, s.item2(p) + 1)
                        prob = buffers(s, "2", p)[1]
                        nc.scalar.activation(prob[:], prob[:], ACT.Exp, scale=SCALE2).then_inc(exp2_done, 1)
                    if s.attn2 and not s.attn1 and p:
                        copy_out("2", pT2, s, p - 1)
                    if s.attn1 and s.attn2 and p:
                        copy_out("1", pT1, s, p)
                    if s.prepare and s.attn2 and p == 1:
                        next_once(s.g + 1)
                    if s.prepare and s.attn2 and p == 2:
                        next_context(s.g + 1)
                if s.attn1 and not s.attn2:
                    copy_out("1", pT1, s, TILES - 1)
                if s.attn2:
                    copy_out("2", pT2, s, TILES - 1)
                if s.attn1:
                    out1(s, TILES - 1)
                if s.prepare:
                    next_twice(s.g + 1)
                if s.attn2:
                    free(s, "O", nc.scalar.copy(o2T[:], take(s, "O")[:]))
                if s.attn1:
                    act.wait_ge(y1_full, s.g + 1)
                    nc.scalar.copy(yT[:], side_y).then_inc(y1_read, 1)
                if s.prepare:
                    free(s, "X", affine(xnT, take(s, "X"), LN_G, LN_B))
                if s.attn2:
                    free(s, "G", affine(h2T, take(s, "G"), LN2_G, LN2_B))
                if s.prepare:
                    free(s, "C", affine(cnT, take(s, "C"), CLN_G, CLN_B))

            run_pipeline(act, body)

            put_filling(act, range(1, EXPERTS, 2))

            def expert_weights(s, slot):
                wait(act, y_ready, s - SLOTS + 1)
                e = act.value_load(block_expert_i[0:1, bass.ds(s, 1)], min_val=0, max_val=EXPERTS - 1)
                nc.scalar.copy(expert_w[slot], expert_all[:, bass.ds(e, 1), :].rearrange("p e n -> p (e n)")).then_inc(
                    expert_w_ready, 1)

            def turned_in(s, slot):
                act.wait_ge(block_turned, s + 1)
                nc.scalar.activation(blockT[slot % 2], turned_bank(slot), ACT.Identity,
                                     bias=vec[:, LN2_B:LN2_B + 1], scale=vec[:, LN2_G:LN2_G + 1]).then_inc(block_T, 1)

            def block_ahead(s, slot, nth):
                if not (isinstance(s, int) and s >= blocks - 1):
                    turned_in(s + 1, (slot + 1) % SLOTS)
                if not (isinstance(s, int) and s >= blocks - 2):
                    expert_weights(s + 2, (slot + 2) % SLOTS)

            act.wait_ge(blocks_ready, 1)
            act.wait_ge(experts_in, 32)
            expert_weights(0, 0)
            expert_weights(1, 1)
            turned_in(0, 0)
            for_blocks(act, block_ahead)

        @block.vector
        def _(dve):
            count = {"base": 0, "n": 0}

            def step(ins):
                count["n"] += 1
                ins.then_inc(dve_done, 1)
                dve.wait_ge(dve_done, count["base"] + count["n"])

            def statistics(which, tiles_of_rows, ready, count):
                for t, rows in enumerate(tiles_of_rows):
                    last = nc.vector.bn_stats(stat[which][:, t, :], rows)
                step(last)
                nc.vector.memset(carrier[:], 0.0)
                for t in range(len(tiles_of_rows)):
                    last = nc.vector.bn_aggr(mv[which][:, t, :], stat[which][:, t, :])
                step(last)
                n = len(tiles_of_rows)
                nc.vector.tensor_scalar(var[which][:, 0:n], mv[which][:, 0:n, 1], EPS, None, ALU.add).then_inc(ready, 1)
                dve.wait_ge(ready, count)

            def tiles_in(rows):
                return [rows[:, t, :] for t in range(TILES)]

            def norm(src, dst, count):
                statistics("rows", tiles_in(src), var_ready, count)
                return normed(src, dst, count)

            def normed(src, dst, count):
                dve.wait_ge(rstd_ready, count)
                for t in range(TILES):
                    last = nc.vector.tensor_scalar(dst[:, t, :], src[:, t, :], mv["rows"][:, t, 0:1],
                                                   rstd["rows"][:, t:t + 1], ALU.subtract, ALU.mult)
                return last

            def next_shift(n, count):
                dve.wait_ge(next_rstd_ready, count)
                nc.vector.scalar_tensor_tensor(out=shift_n["next"][:, 0:n], in0=mv["next"][:, 0:n, 0], scalar=-1.0,
                                               in1=rstd["next"][:, 0:n], op0=ALU.mult,
                                               op1=ALU.mult).then_inc(next_shift_ready, 1)
                dve.wait_ge(next_shift_ready, count)

            def next_first(g):
                wait(dve, next_rows, 2 * g)
                statistics("next", tiles_in(group_rows(x_s, g)) + tiles_in(group_rows(c_s, g)), next_var_ready,
                           2 * g + 1)

            def next_second(g):
                dve.wait_ge(x_once, g + 1)
                dve.wait_ge(next_rows, 2 * g + 1)
                statistics("next", tiles_in(xh), next_var_ready, 2 * g + 2)

            def less_max(score, mx, prob, free_sem):
                step(nc.vector.reduce_max(mx, score[:], AX_X))
                nc.vector.tensor_tensor(prob[:], score[:], mx[:, :, None].to_broadcast([P, HEADS, SEQ]),
                                        ALU.subtract).then_inc(free_sem, 1)

            def invert_sum(prob, sm, inv, ready):
                step(nc.vector.reduce_sum(sm[:], prob[:], AX_X))
                nc.vector.reciprocal(inv, sm[:]).then_inc(ready, 1)

            dve.wait_ge(rows0_in, 32)
            next_first(0)
            next_shift(2 * TILES, 1)
            next_second(0)
            next_shift(TILES, 2)
            def split(whole, hi, lo, count):
                nc.vector.tensor_copy(hi[:], whole).then_inc(hi_done, 1)
                dve.wait_ge(hi_done, count)
                nc.vector.tensor_tensor(lo[:], whole, hi[:].bitcast(F32), ALU.subtract).then_inc(weights_split, 1)

            dve.wait_ge(queries_in, 32)
            split(wq1_s, wq1_hi, wq1_lo, 1)
            split(wff1_s, wff1_hi, wff1_lo, 2)

            def split_x(s, name):
                wait_read(dve, s, name)
                step(nc.vector.tensor_copy(xnT_hi[:], xnT[:]))
                nc.vector.tensor_tensor(xnT_lo[:], xnT[:], xnT_hi[:].bitcast(F32), ALU.subtract).then_inc(
                    xnT_lo_ready, 1)

            def values2_in(s):
                for half, name in enumerate(("v2a", "v2b")):
                    dve.wait_ge(bank_full[s.bank(name)], s.full(name))
                    bank = shared[s.bank(name)][:].rearrange("p (b h c d) -> p b h c d", b=GB // 2, h=HP, c=2)
                    bias = bv_s[:].rearrange("p (h c d) -> p h c d", h=HP, c=2)
                    to = v2block[:, half * GB // 2:(half + 1) * GB // 2, 0:HP, :, 0:D2]
                    for c in range(2):
                        rows = slice(c * SEQ, (c + 1) * SEQ)
                        last = nc.vector.tensor_tensor(
                            to[rows, :, :, c, :], bank[rows, :, :, c, :],
                            bias[rows, None, :, c, :].to_broadcast([SEQ, GB // 2, HP, D2]), ALU.add)
                    last.then_inc(bank_free[s.bank(name)], 1)

            def out2(s, p):
                dve.wait_ge(bank_full[s.bank(f"o2{p}")], s.full(f"o2{p}"))
                bank = shared[s.bank(f"o2{p}")][:, 0:HP * PER_TILE * 2 * (D2 + 1)].rearrange(
                    "p (h b c d) -> p h b c d", h=HP, b=PER_TILE, c=2)
                inv = inv2[:, p % 2].rearrange("p (h c) -> p h c", h=HP)
                to = o2[:, p, :].rearrange("p (h c d) -> p h c d", h=HP, c=2)
                for b in range(PER_TILE):
                    rows = slice(b * SEQ, (b + 1) * SEQ)
                    last = nc.vector.reciprocal(inv[rows], bank[rows, :, b, :, D2])
                step(last)
                for b in range(PER_TILE):
                    rows = slice(b * SEQ, (b + 1) * SEQ)
                    last = nc.vector.tensor_tensor(to[rows], bank[rows, :, b, :, 0:D2],
                                                   inv[rows][:, :, :, None].to_broadcast([SEQ, HP, 2, D2]), ALU.mult)
                last.then_inc(bank_free[s.bank(f"o2{p}")], 1)

            def gated(s, p):
                dve.wait_ge(tanh_done, s.item1(p) + 1)
                fg, fh = s.bank(f"fg{p}"), s.bank(f"fh{p}")
                ins = nc.vector.scalar_tensor_tensor(out=tanh_g[:], in0=tanh_g[:], scalar=1.0,
                                                     in1=shared[fg][:], op0=ALU.add, op1=ALU.mult)
                ins.then_inc(bank_free[fg], 1)
                wait_read(dve, s, f"fg{p}")
                dve.wait_ge(bank_full[fh], s.full(f"fh{p}"))
                ins = nc.vector.tensor_tensor(ffT[:, p, :], tanh_g[:], shared[fh][:], ALU.mult)
                ins.then_inc(bank_free[fh], 1)

            def choose(s):
                dve.wait_ge(logits_full, s.g - 1)
                step(nc.vector.tensor_tensor(
                    logits[:], side_router[:, 0:TILES * EXPERTS].rearrange("p (t e) -> p t e", t=TILES),
                    gb_s[:, None, :].to_broadcast([P, TILES, EXPERTS]), ALU.add))
                over = lmax[:, :, None].to_broadcast([P, TILES, EXPERTS])
                step(nc.vector.reduce_max(lmax[:], logits[:], AX_X))
                step(nc.vector.tensor_tensor(chosen, logits[:], over, ALU.is_equal))
                step(nc.vector.tensor_tensor(chosen, chosen, first_wins[:, None, :].to_broadcast([P, TILES, EXPERTS]),
                                             ALU.mult))
                step(nc.vector.reduce_max(lmax[:], chosen, AX_X))
                nc.vector.tensor_tensor(chosen, chosen, over, ALU.is_equal).then_inc(chosen_ready, 1)

            def positions(s):
                dve.wait_ge(ranks_read, s.g - 1)
                dve.wait_ge(chosen_ready, s.g - 1)
                for t in range(TILES):
                    step(nc.vector.tensor_tensor(next_at[:, t + 1], next_at[:, t], rank_count[:, 1, t], ALU.add))
                step(nc.vector.tensor_tensor(spots[:], next_at[:, 0:TILES], rank_count[:, 0], ALU.add))
                step(nc.vector.tensor_tensor(spots[:], spots[:], chosen, ALU.mult))
                step(nc.vector.reduce_sum(position[:], spots[:], AX_X))
                nc.vector.tensor_copy(position_i[:], position[:]).then_inc(positions_ready, 1)
                step(nc.vector.tensor_copy(next_at[:, 0], next_at[:, TILES]))

            def body(s):
                if not (s.attn1 or s.attn2):
                    choose(s)
                    positions(s)
                    return
                if s.attn2:
                    g = s.g - 1
                    dve.wait_ge(bank_full[s.bank("Y")], s.full("Y"))
                    ins = nc.vector.tensor_tensor(x1[:], group_rows(x_s, g),
                                                  shared[s.bank("Y")][:].rearrange("p (t d) -> p t d", t=TILES),
                                                  ALU.add)
                    ins.then_inc(bank_free[s.bank("Y")], 1)
                    wait_read(dve, s, "Y")
                    statistics("rows", tiles_in(x1), var_ready, 3 * g + 1)
                    if s.route:
                        choose(s)
                    step(normed(x1, z, 3 * g + 1))
                    norm(z, hn, 3 * g + 2).then_inc(hn_ready, 1)
                    dve.wait_ge(hn_ready, s.g)
                    step(nc.vector.tensor_tensor(z[:], z[:], bo_s[:, None, :].to_broadcast([P, TILES, P]), ALU.add))
                if s.prepare and not s.attn2:
                    split_x(s, "X0")
                    dve.wait_ge(rows_in, 32)
                    dve.wait_ge(const_ready, 1)
                if s.prepare:
                    next_first(s.g + 1)
                if s.prepare and not s.attn2:
                    next_shift(2 * TILES, 2 * s.g + 3)
                    dve.wait_ge(weights_in, WEIGHTS_IN)
                    nc.vector.tensor_scalar(wff2_s[:], wff2_s[:], 0.5, None, ALU.mult).then_inc(half_w, 1)
                for p in range(TILES):
                    if s.attn1:
                        dve.wait_ge(score1_full, s.item1(p) + 1)
                        score, prob = buffers(s, "1", p)
                        less_max(score, max1[:, p % 2], prob, score1_free)
                    if s.attn1 and (p or not s.attn2):
                        gated(s, p)
                    if s.attn2 and p == 0:
                        values2_in(s)
                    if s.attn1:
                        dve.wait_ge(exp1_done, s.item1(p) + 1)
                        invert_sum(prob, sum1, inv1[:, p % 2], inv1_ready)
                    if s.attn1 and s.attn2 and p == 0:
                        gated(s, p)
                    if s.prepare and s.attn2 and p == 0:
                        next_shift(2 * TILES, 2 * s.g + 3)
                    if s.attn2:
                        dve.wait_ge(score2_full, s.item2(p) + 1)
                        score, prob = buffers(s, "2", p)
                        less_max(score, max2[:, p % 2], prob, score2_free)
                        if s.attn1 and p:
                            out2(s, p - 1)
                        if not s.attn1 and p > 1:
                            out2(s, p - 2)
                if s.prepare:
                    next_second(s.g + 1)
                if s.route:
                    positions(s)
                if s.prepare:
                    next_shift(TILES, 2 * s.g + 4)
                if s.attn2 and not s.attn1:
                    out2(s, TILES - 2)
                if s.attn2:
                    out2(s, TILES - 1)
                    g = s.g - 1
                    dve.wait_ge(bank_full[s.bank("P")], s.full("P"))
                    ins = nc.vector.tensor_tensor(z[:], z[:], shared[s.bank("P")][:].rearrange(
                        "p (t d) -> p t d", t=TILES), ALU.add)
                    ins.then_inc(bank_free[s.bank("P")], 1)
                    wait_read(dve, s, "P")
                    wait(dve, scattered, 16 * TILES * (s.g - 1))
                    norm(z, rows_out[:, :, RN:RN + P], 3 * g + 3).then_inc(h2_ready, 1)
                    dve.wait_ge(h2_ready, s.g)
                    step(nc.vector.tensor_scalar(rows_out[:, :, RI], rows_out[:, :, RI], float(GT), None, ALU.add))
                    step(nc.vector.tensor_tensor(rows_out[:, :, RT:RT + P], x1[:], z[:], ALU.add))
                if s.prepare:
                    split_x(s, "X")

            body(first_step())
            body(second_step())
            first_end = count["n"]
            per_middle = MIDDLE_VECTOR_STEPS
            with dve.Fori(2, groups - 1) as g:
                count["base"], count["n"] = (g - 2) * per_middle + first_end, 0
                body(middle_step(g))
                assert count["n"] == per_middle, f"MIDDLE_VECTOR_STEPS is {count['n']}"
            count["base"], count["n"] = 0, first_end + (groups - 3) * per_middle
            body(last_step())
            body(drain_step())
            body(route_step())

            nc.vector.tensor_copy(filling_at[:], next_at[:, 0]).then_inc(filling_at_ready, 1)
            step(nc.vector.tensor_tensor(rows_of[:], next_at[:, 0], room_at[:], ALU.subtract))
            step(nc.vector.tensor_tensor(compare, starts[:, None, :].to_broadcast([P, EXPERTS, blocks]),
                                         rows_of[:, :, None].to_broadcast([P, EXPERTS, blocks]), ALU.is_lt))
            step(nc.vector.reduce_sum(padded[:], compare, AX_X))
            step(nc.vector.tensor_scalar(padded[:], padded[:], float(BLOCK), None, ALU.mult))
            step(nc.vector.tensor_tensor_scan(padded_end[:], ones[:, 0:EXPERTS], padded[:], 0.0, ALU.mult, ALU.add))
            step(nc.vector.tensor_tensor(compare_b, padded_end[:, None, :].to_broadcast([P, blocks, EXPERTS]),
                                         starts[:, :, None].to_broadcast([P, blocks, EXPERTS]), ALU.is_le))
            step(nc.vector.tensor_scalar(padded[:], padded[:], -1.0, float(room), ALU.mult, ALU.add))
            step(nc.vector.tensor_tensor(jumps, compare_b[:], padded[:, None, :].to_broadcast([P, blocks, EXPERTS]),
                                         ALU.mult))
            step(nc.vector.reduce_sum(block_at[:], jumps, AX_X))
            step(nc.vector.tensor_tensor(block_at[:], block_at[:], starts[:], ALU.add))
            step(nc.vector.tensor_scalar(block_at_i[:], block_at[:], float(idle_at), None, ALU.min))
            step(nc.vector.reduce_sum(block_expert[:], compare_b, AX_X))
            nc.vector.tensor_scalar(block_expert_i[:], block_expert[:], float(EXPERTS - 1), None,
                                    ALU.min).then_inc(blocks_ready, 1)

            def experts_mid(s, slot, nth):
                w = expert_w[slot]
                dve.wait_ge(block_in[slot], 16 * nth)
                if not (isinstance(s, int) and s < SLOTS):
                    dve.wait_ge(out_stored[slot], 16 * BA * (nth - 1))
                nc.vector.tensor_copy(token_i[:, slot], block_rows[slot][:, :, RI])
                for c in range(FC):
                    if c % 2 == 0:
                        dve.wait_ge(mid_full, 2 * s + c // 2 + 1)
                    nc.vector.tensor_scalar(mid[slot % 2][:, c, :], mid_bank(slot % 2, c), w[:, EB1 + c:EB1 + c + 1],
                                            0.0, ALU.add, ALU.max).then_inc(mid_ready, 1)
                if not (isinstance(s, int) and s == 0):
                    output(s - 1, (slot - 1) % SLOTS)

            def output(s, slot):
                dve.wait_ge(rest_ready, s + 1)
                dve.wait_ge(y_full, s + 1)
                nc.vector.tensor_tensor(y_rows[slot], y_bank(slot).rearrange("p (a d) -> p a d", a=BA),
                                        block_rows[slot][:, :, RT:RT + P], ALU.add).then_inc(y_ready, 1)

            for_blocks(dve, experts_mid)
            output(blocks - 1, (blocks - 1) % SLOTS)

        @block.tensor
        def _(pe):
            def claim(s, name):
                b = s.bank(name)
                wait(pe, bank_free[b], s.full(name) - 1)
                return shared[b]

            def done(s, name, ins):
                ins.then_inc(bank_full[s.bank(name)], 1)

            def turn(bank, rows):
                for t in range(TILES):
                    last = nc.tensor.transpose(bank[:, t * P:(t + 1) * P], rows[:, t, :], ident[:])
                return last

            def mm(to, lhsT, rhs, start=True, stop=True):
                return nc.tensor.matmul(to, lhsT, rhs, start=start, stop=stop)

            def mm_x(bank, hi, lo, at):
                mm(bank[:], hi[:, at:at + P], xnT_hi[:], stop=False)
                mm(bank[:], hi[:, at:at + P], xnT_lo[:], start=False, stop=False)
                return mm(bank[:], lo[:, at:at + P], xnT_hi[:], start=False)

            def rows_twice(to, T, b, w):
                for half in range(2):
                    last = mm(to[half * SEQ:(half + 1) * SEQ], T[:, b * SEQ:(b + 1) * SEQ], w)
                return last

            def scores1(s, p):
                score = buffers(s, "1", p)[0]
                wait(pe, score1_free, s.item1(p) - (0 if s.attn2 else 1))
                for h in range(HP):
                    if p == 0 and h >= HP - 2:
                        wait_read(pe, s, f"Q{h}")
                    for b in range(PER_TILE):
                        at = p * P + b * SEQ
                        last = mm(score[b * SEQ:(b + 1) * SEQ, 2 * h:2 * h + 2, :], qT[:, h, at:at + SEQ],
                                  kblock[:, PER_TILE * p + b])
                last.then_inc(score1_full, 1)

            def scores2(s, p):
                score = buffers(s, "2", p)[0]
                wait(pe, score2_free, s.item2(p) - (0 if s.attn1 else 1))
                if s.route and not s.attn1:
                    pe.wait_ge(ranks_read, s.g - 1)
                pe.wait_ge(spread_ready, s.item2(p) + 1)
                for half in range(2):
                    for b in range(PER_TILE):
                        at = p * P + b * SEQ
                        hs = slice(half * HEADS // 2, (half + 1) * HEADS // 2)
                        last = mm(score[b * SEQ:(b + 1) * SEQ, hs, :], q2T[:, at:at + SEQ],
                                  kspread[:, p % 2, b, hs, :])
                last.then_inc(score2_full, 1)

            def turn_probs(which, s, p):
                prob = buffers(s, which, p)[1]
                ready, item = (prob1_ready, s.item1(p)) if which == "1" else (exp2_done, s.item2(p))
                pe.wait_ge(ready, item + 1)
                wait(pe, tr_free, tr_index(s, which, p))
                for h in range(HP):
                    last = nc.tensor.transpose(transposed[:, h, :], prob[:, 2 * h:2 * h + 2, :], ident[:])
                last.then_inc(tr_full, 1)

            def values1(s, p):
                pe.wait_ge(tr_free, tr_index(s, "1", p) + 1)
                for b in range(PER_TILE):
                    name = f"o1{'ab'[b]}{p}"
                    bank = claim(s, name)
                    done(s, name, mm(bank[:], vblock[:, PER_TILE * p + b], pT1[:, :, b * SEQ:(b + 1) * SEQ]))

            def values2(s, p):
                if p == 0:
                    for name in ("v2a", "v2b"):
                        wait_read(pe, s, name)
                pe.wait_ge(tr_free, tr_index(s, "2", p) + 1)
                bank = claim(s, f"o2{p}")
                own = PER_TILE * 2 * (D2 + 1)
                for h in range(HP):
                    last = mm(bank[:, h * own:(h + PAIRS) * own], pT2[:, h, :],
                              v2block[:, PER_TILE * p:PER_TILE * (p + 1), h:h + PAIRS].rearrange(
                                  "p b h c d -> p h b (c d)"))
                done(s, f"o2{p}", last)

            pe.wait_ge(const_ready, 1)
            pe.wait_ge(next_rows, 1)
            turn(shared[1], ch).then_inc(bank_full[1], 1)
            pe.wait_ge(context_in, CONTEXT_IN)

            def body(s):
                def ranks():
                    pe.wait_ge(chosen_ready, s.g - 1)
                    mm(side_router[:, 0:WIDE], below[:], chosen_wide[:])
                    mm(side_router[:, WIDE:2 * WIDE], ones[:, 0:P], chosen_wide[:]).then_inc(ranks_full, 1)

                if s.attn2:
                    if not s.attn1:
                        for b in range(2):
                            pe.wait_ge(bank_free[b], s.used[b])
                    pe.wait_ge(y1_read, s.g)
                    done(s, "Y", turn(claim(s, "Y"), yT[:].rearrange("p (t d) -> p t d", t=TILES)))
                if s.attn1:
                    for b in range(2):
                        wait(pe, bank_free[b], s.used[b])
                    done(s, "K", mm(claim(s, "K")[:], wk1_s[:].rearrange("p a d -> p (a d)"), cnT[:]))
                    bank = claim(s, "V")
                    for b in range(GB):
                        last = rows_twice(bank[:, b * D1:(b + 1) * D1], cnT, b, wv1_s[:])
                    done(s, "V", last)
                    if not s.attn2:
                        pe.wait_ge(next_rows, 2)
                        done(s, "X0", turn(claim(s, "X0"), xh))
                        wait_read(pe, s, "X0")
                        pe.wait_ge(weights_split, 2)
                    for h in range(HP):
                        if s.route and h == RANKS_AT:
                            ranks()
                        if h == 0:
                            pe.wait_ge(xnT_lo_ready, s.g + 1)
                        done(s, f"Q{h}", mm_x(claim(s, f"Q{h}"), wq1_hi, wq1_lo, h * P))
                elif s.route:
                    ranks()
                if not (s.attn1 or s.attn2):
                    pe.wait_ge(ranks_read, s.g - 1)
                    return
                if s.attn2:
                    pe.wait_ge(hn_ready, s.g)
                    done(s, "H", turn(claim(s, "H"), hn))
                if s.attn1 and s.attn2:
                    pe.wait_ge(y1_read, s.g)
                if s.attn1 and s.route:
                    pe.wait_ge(ranks_read, s.g - 1)

                def project2():
                    wait_read(pe, s, "H")
                    done(s, "k2", mm(claim(s, "k2")[:], wk2_s[:], hnT[:]))
                    done(s, "q2", mm(claim(s, "q2")[:], wq2_s[:], hnT[:]))
                    for half, name in enumerate(("v2a", "v2b")):
                        bank = claim(s, name)
                        for b in range(GB // 2):
                            last = rows_twice(bank[:, b * P:(b + 1) * P], hnT, half * GB // 2 + b, wv2_s[:])
                        done(s, name, last)

                alone = not (s.attn1 and s.attn2)
                if s.attn1 and alone:
                    scores1(s, 0)
                    pe.wait_ge(weights_in, WEIGHTS_IN)
                    pe.wait_ge(half_w, 1)
                for p in range(TILES):
                    if s.attn1 and not alone:
                        scores1(s, p)
                    if s.attn2 and p == 0:
                        project2()
                    if s.attn1:
                        for name, at in ((f"fg{p}", FF), (f"fh{p}", 0)):
                            done(s, name, mm_x(claim(s, name), wff1_hi, wff1_lo, at + p * P))
                    if s.attn1 and alone:
                        if p:
                            turn_probs("1", s, p - 1)
                        if p + 1 < TILES:
                            scores1(s, p + 1)
                    if s.attn2 and p and not alone:
                        turn_probs("2", s, p - 1)
                    if s.attn2:
                        scores2(s, p)
                    if s.attn1 and p:
                        values1(s, p - 1)
                    if s.attn2 and p and not alone:
                        values2(s, p - 1)
                    if s.attn2 and alone:
                        if p > 1:
                            values2(s, p - 2)
                        if p:
                            turn_probs("2", s, p - 1)
                    if s.attn1 and not alone:
                        turn_probs("1", s, p)
                if s.attn2 and alone:
                    values2(s, TILES - 2)
                def w_part(chunks):
                    if s.attn1:
                        for c in chunks:
                            lhsT, rhs = (wff2_s[:, c, :], ffT[:, c, :]) if c < FC else \
                                (wo1_s[:, c - FC, :], oT[:, c - FC, :])
                            last = mm(side_y, lhsT, rhs, start=(c == 0), stop=(c == FC + HP - 1))
                        if chunks[-1] == FC + HP - 1:
                            last.then_inc(y1_full, 1)

                if s.attn1:
                    pe.wait_ge(score1_free, s.item1(TILES))
                    wait_read(pe, s, f"fh{TILES - 1}")
                w_part(range(0, FC))
                if s.attn1 and alone:
                    turn_probs("1", s, TILES - 1)
                if s.attn2:
                    turn_probs("2", s, TILES - 1)
                if s.attn1:
                    values1(s, TILES - 1)
                if s.attn2:
                    values2(s, TILES - 1)
                if s.attn1:
                    for name in (f"o1a{TILES - 1}", f"o1b{TILES - 1}"):
                        wait_read(pe, s, name)
                w_part(range(FC, FC + 2))
                if s.attn2:
                    wait_read(pe, s, f"o2{TILES - 1}")
                    done(s, "O", turn(claim(s, "O"), o2))
                w_part(range(FC + 2, FC + 3))
                if s.attn2:
                    wait_read(pe, s, "O")
                    bank = claim(s, "P")
                    for t in range(TILES):
                        last = mm(bank[:, t * P:(t + 1) * P], o2T[:, t * P:(t + 1) * P], wo2_s[:])
                    done(s, "P", last)
                w_part(range(FC + 3, FC + HP))
                if s.prepare:
                    pe.wait_ge(next_rows, 2 * s.g + 4)
                    done(s, "X", turn(claim(s, "X"), xh))
                if s.attn2:
                    pe.wait_ge(h2_ready, s.g)
                    done(s, "G", turn(claim(s, "G"), rows_out[:, :, RN:RN + P]))
                if s.prepare:
                    done(s, "C", turn(claim(s, "C"), ch))
                if s.attn2:
                    wait_read(pe, s, "G")
                    if s.route:
                        pe.wait_ge(ranks_read, s.g - 1)
                    for t in range(TILES):
                        last = mm(side_router[:, t * EXPERTS:t * EXPERTS + WIDE], h2T[:, t * P:(t + 1) * P], gw_s[:])
                    last.then_inc(logits_full, 1)

            run_pipeline(pe, body)

            def turn_block(s, slot, nth):
                pe.wait_ge(block_in[slot], 16 * nth)
                wait(pe, block_T, s - 1)
                for a in range(BA):
                    last = nc.tensor.transpose(turned_bank(slot)[:, a * P:(a + 1) * P], block_rows[slot][:, a, RN:RN + P],
                                               ident[:])
                last.then_inc(block_turned, 1)

            def output(s, slot):
                wait(pe, y_ready, s - 1)
                w = expert_w[slot]
                for a in range(BA):
                    for c in range(FC):
                        if a == 0:
                            pe.wait_ge(mid_ready, FC * s + c + 1)
                        last = mm(y_bank(slot)[:, a * P:(a + 1) * P], mid[slot % 2][:, c, a * P:(a + 1) * P],
                                  w[:, EW2 + c * P:EW2 + (c + 1) * P], start=(c == 0), stop=(c == FC - 1))
                last.then_inc(y_full, 1)

            def one_block(s, slot, nth):
                if not (isinstance(s, int) and s == blocks - 1):
                    turn_block(s + 1, (slot + 1) % SLOTS, nth + (slot + 1) // SLOTS)
                pe.wait_ge(expert_w_ready, s + 1)
                pe.wait_ge(block_T, s + 1)
                wait(pe, mid_ready, FC * (s - 1))
                w = expert_w[slot]
                for c in range(FC):
                    last = mm(mid_bank(slot % 2, c), w[:, EW1 + c * P:EW1 + (c + 1) * P], blockT[slot % 2])
                    if c % 2:
                        last.then_inc(mid_full, 1)
                if not (isinstance(s, int) and s == 0):
                    output(s - 1, (slot - 1) % SLOTS)

            turn_block(0, 0, 1)
            for_blocks(pe, one_block)
            output(blocks - 1, (blocks - 1) % SLOTS)


def kernel(**inputs):
    import numpy as np

    import concourse.bacc as bacc
    from concourse.bass_utils import run_bass_kernel_spmd

    a = {k: np.asarray(v) for k, v in inputs.items()}
    f = {k[len("L0_ffn_"):]: v for k, v in a.items() if k.startswith("L0_ffn_")}
    c = {k[len("L0_xattn_"):]: v for k, v in a.items() if k.startswith("L0_xattn_")}
    shape = a["x"].shape
    width = shape[-1]
    w2 = f["w2"].reshape(EXPERTS, FC, P, P).transpose(0, 2, 1, 3).reshape(EXPERTS, P, FC * P)
    b1 = f["b1"].reshape(EXPERTS, FC, P).transpose(0, 2, 1)
    b2 = np.broadcast_to(f["b2"][:, None, :], (EXPERTS, P, P))
    experts = np.concatenate([f["w1"], w2, b1, b2], axis=2)
    laid = {
        "x": a["x"].reshape(-1, width), "ctx": a["ctx_1024"].reshape(-1, width),
        "wq1": c["Wq"], "wk1": c["Wkv"][:, :D1], "wv1": c["Wkv"][:, D1:], "wo1": c["Wo"],
        "wff1": c["Wff1"], "wff2": c["Wff2"], "wq2": f["wq"], "wk2": f["wk"], "wv2": f["wv"], "wo2": f["wo"],
        "vectors": np.stack([c["ln_g"], c["ln_b"], c["cln_g"], c["cln_b"], f["ln1_g"], f["ln1_b"], f["ln2_g"],
                             f["ln2_b"], f["bq"], f["bk"]], axis=1),
        "bv": f["bv"], "bo": f["bo"], "gate_w": f["gate_w"], "gate_b": f["gate_b"], "experts": experts,
    }
    nc = bacc.Bacc("TRN2", target_bir_lowering=False, num_devices=1)
    arrays, args = {}, []
    for name, v in laid.items():
        v = np.ascontiguousarray(v)
        arrays[f"in_{name}"] = v
        args.append(nc.dram_tensor(f"in_{name}", v.shape, mybir.dt.from_np(v.dtype), kind="ExternalInput").ap())
    args.append(nc.dram_tensor("out_x", arrays["in_x"].shape, F32, kind="ExternalOutput").ap())
    build(nc, *args)
    r = run_bass_kernel_spmd(nc, [arrays], core_ids=[0])
    return r.results[0]["out_x"].reshape(shape)
```
